# Optimizing a Trainium2 kernel written in Bass

```python
import numpy as np
import jax
import jax.numpy as jnp

def _softmax(x, axis=-1):
    return jax.nn.softmax(x, axis=axis)

def _gelu(x):
    return jax.nn.gelu(x, approximate=True)

def _silu(x):
    return jax.nn.silu(x)

def _sigmoid(x):
    return jax.nn.sigmoid(x)

def _layernorm(x, axis=-1, eps=1e-05):
    m = jnp.mean(x, axis=axis, keepdims=True)
    v = jnp.var(x, axis=axis, keepdims=True)
    return (x - m) / jnp.sqrt(v + eps)

def _scatter_add(tgt, idx, src, axis=0):
    return tgt.at[idx].add(src)

def _segment_sum(src, seg, n):
    return jax.ops.segment_sum(src, seg, n)
kernel_name = 'mk_flamingo_gated_d1_seqx_r8_5aaaec'

def setup_inputs(seed: int=0):
    np.random.seed(seed)
    _w = jnp.asarray

    def _rec_inputs():
        import jax
        import jax.numpy as jnp
        _rk = jax.random.key(seed)
        x = 7.22e-05 + 1 * jax.random.normal(jax.random.fold_in(_rk, 1), (32, 64, 512), jnp.float32)
        _lenS = 64 - jax.random.randint(jax.random.fold_in(_rk, 7), (32,), 0, max(1, 64 // 4) + 1, jnp.int32)
        _lenS2 = 64 - jax.random.randint(jax.random.fold_in(_rk, 8), (32,), 0, max(1, 64 // 4) + 1, jnp.int32)
        _ctx_4096P = jax.random.normal(jax.random.fold_in(_rk, 11), (32, 16, 512), jnp.float32)
        _ctx_4096c = jax.random.dirichlet(jax.random.fold_in(_rk, 511), 0.3 * jnp.ones((16,), jnp.float32), (32, 64))
        _ctx_4096t = jnp.einsum('bsk,bkd->bsd', _ctx_4096c, _ctx_4096P)
        _ctx_4096t = _ctx_4096t * jax.lax.rsqrt(jnp.mean(jnp.square(_ctx_4096t)) + 1e-12) * 0.953939
        ctx_4096 = 4.13588e-05 + 0.999923 * (_ctx_4096t + 0.3 * jax.random.normal(jax.random.fold_in(_rk, 611), (32, 64, 512), jnp.float32))
        fside_Bx32xSxS2_0 = 1.74963e-06 + 0.0200011 * jax.random.normal(jax.random.fold_in(_rk, 13), (32, 32, 64, 64), jnp.float32)
        _validS = jnp.arange(64)[None, :] < _lenS[:, None]
        _validS2 = jnp.arange(64)[None, :] < _lenS2[:, None]
        _causal = jnp.tril(jnp.ones((64, 64), dtype=bool))
        mask_BxSxS2_bk0 = jnp.logical_not(jnp.broadcast_to(_validS2[:, None, :], (32, 64, 64)))
        _g = jax.random.normal(jax.random.fold_in(_rk, 9001), (2, 1), jnp.float32)
        _g = jnp.sign(_g) * jnp.maximum(jnp.abs(_g), 1.0) + (_g == 0) * 1.0
        g_xattn = _g[0]
        g_ffn = _g[1]
        return (x, ctx_4096, fside_Bx32xSxS2_0, mask_BxSxS2_bk0, g_xattn, g_ffn)
    x, ctx_4096, fside_Bx32xSxS2_0, mask_BxSxS2_bk0, g_xattn, g_ffn = _rec_inputs()

    def _L0_xattn_setup():
        import jax, jax.numpy as jnp
        import numpy as np
        B, S, D, H, DH = (2, 128, 512, 32, 128)
        key = jax.random.key(seed)
        ks = jax.random.split(key, 7)
        hidden_q = jax.random.normal(ks[0], (B, S, D), dtype=jnp.float32)
        hidden_kv = jax.random.normal(ks[1], (B, S, D), dtype=jnp.float32)
        attention_mask = jnp.tril(jnp.ones((B, S, S), dtype=bool))
        position_bias = jax.random.normal(ks[2], (B, H, S, S), dtype=jnp.float32) * 0.02
        Wq = jax.random.normal(ks[3], (D, H * DH), dtype=jnp.float32) * 0.02
        Wk = jax.random.normal(ks[4], (D, H * DH), dtype=jnp.float32) * 0.02
        Wv = jax.random.normal(ks[5], (D, H * DH), dtype=jnp.float32) * 0.02
        Wo = jax.random.normal(ks[6], (H * DH, D), dtype=jnp.float32) * 0.02
        return {'hidden_q': hidden_q, 'hidden_kv': hidden_kv, 'attention_mask': attention_mask, 'position_bias': position_bias, 'Wq': Wq, 'Wk': Wk, 'Wv': Wv, 'Wo': Wo}
    _L0_xattn_all = _L0_xattn_setup()
    _L0_xattn_in = {k: v for k, v in _L0_xattn_all.items() if k in ('Wq', 'Wk', 'Wv', 'Wo')}
    del _L0_xattn_all

    def _L0_ffn_setup():
        import jax, jax.numpy as jnp
        import numpy as np
        DIM = 512
        INTER = 1792
        SPARSITY = 32
        RANK = 16
        key = jax.random.key(seed)
        ks = jax.random.split(key, 5)
        B, T = (32, 1)
        x = jax.random.normal(ks[0], (B, T, DIM), dtype=jnp.float32)
        c1_w = jax.random.normal(ks[1], (RANK, DIM), dtype=jnp.float32) * (1.0 / np.sqrt(DIM))
        c2_w = jax.random.normal(ks[2], (INTER, RANK), dtype=jnp.float32) * (1.0 / np.sqrt(RANK))
        w1 = jax.random.normal(ks[3], (INTER, DIM), dtype=jnp.float32) * (1.0 / np.sqrt(DIM))
        w2t = jax.random.normal(ks[4], (INTER, DIM), dtype=jnp.float32) * (1.0 / np.sqrt(INTER))
        return {'x': x, 'c1_w': c1_w, 'c2_w': c2_w, 'w1': w1, 'w2t': w2t}
    _L0_ffn_all = _L0_ffn_setup()
    _L0_ffn_in = {k: v for k, v in _L0_ffn_all.items() if k in ('c1_w', 'c2_w', 'w1', 'w2t')}
    del _L0_ffn_all
    return {'x': x, 'ctx_4096': ctx_4096, 'fside_Bx32xSxS2_0': fside_Bx32xSxS2_0, 'mask_BxSxS2_bk0': mask_BxSxS2_bk0, 'g_xattn': g_xattn, 'g_ffn': g_ffn, 'L0_xattn_Wq': _L0_xattn_in['Wq'], 'L0_xattn_Wk': _L0_xattn_in['Wk'], 'L0_xattn_Wv': _L0_xattn_in['Wv'], 'L0_xattn_Wo': _L0_xattn_in['Wo'], 'L0_ffn_c1_w': _L0_ffn_in['c1_w'], 'L0_ffn_c2_w': _L0_ffn_in['c2_w'], 'L0_ffn_w1': _L0_ffn_in['w1'], 'L0_ffn_w2t': _L0_ffn_in['w2t']}

def reference(x, ctx_4096, fside_Bx32xSxS2_0, mask_BxSxS2_bk0, g_xattn, g_ffn, L0_xattn_Wq, L0_xattn_Wk, L0_xattn_Wv, L0_xattn_Wo, L0_ffn_c1_w, L0_ffn_c2_w, L0_ffn_w1, L0_ffn_w2t):
    import jax
    import jax.numpy as jnp

    def _L0_xattn_ref(hidden_q, hidden_kv, attention_mask, position_bias, Wq, Wk, Wv, Wo):
        import jax, jax.numpy as jnp
        import numpy as np
        B, S, D, H, DH = (2, 128, 512, 32, 128)
        b, lq, _ = hidden_q.shape
        lk = hidden_kv.shape[1]
        h, dh = (H, DH)
        q = (hidden_q @ Wq).reshape(b, lq, h, dh)
        k = (hidden_kv @ Wk).reshape(b, lk, h, dh)
        v = (hidden_kv @ Wv).reshape(b, lk, h, dh)
        scale = 1.0 / jnp.sqrt(jnp.asarray(dh, dtype=q.dtype))
        score = jnp.einsum('bqhd,bkhd->bhqk', q, k) * scale + position_bias
        mask = attention_mask[:, None, :, :]
        neg_inf = jnp.asarray(-jnp.inf, dtype=score.dtype)
        score = jnp.where(mask, score, neg_inf)
        probs = jax.nn.softmax(score, axis=-1)
        probs = jnp.where(mask, probs, jnp.asarray(0, dtype=probs.dtype))
        ctx = jnp.einsum('bhqk,bkhd->bqhd', probs, v).reshape(b, lq, h * dh)
        return ctx @ Wo

    def _L0_ffn_ref(x, c1_w, c2_w, w1, w2t):
        import jax, jax.numpy as jnp
        import numpy as np
        DIM = 512
        INTER = 1792
        SPARSITY = 32
        RANK = 16
        B, T, M = x.shape
        xf = x.reshape(B * T, M)
        inter = xf @ c1_w.T @ c2_w.T
        n_blocks = INTER // SPARSITY
        blk = inter.reshape(B * T, n_blocks, SPARSITY)
        idx = jnp.argmax(blk, axis=-1) + jnp.arange(0, INTER, SPARSITY)
        w1_g = w1[idx]
        w2_g = w2t[idx]
        h = jax.nn.relu(jnp.einsum('bkm,bm->bk', w1_g, xf))
        out = jnp.einsum('bk,bkm->bm', h, w2_g)
        return out.reshape(B, T, M)
    x = x + jnp.tanh(g_xattn[0]) * _L0_xattn_ref(_layernorm(x, axis=-1), ctx_4096, mask_BxSxS2_bk0, fside_Bx32xSxS2_0, L0_xattn_Wq, L0_xattn_Wk, L0_xattn_Wv, L0_xattn_Wo)
    x = x + jnp.tanh(g_ffn[0]) * _L0_ffn_ref(_layernorm(x, axis=-1), L0_ffn_c1_w, L0_ffn_c2_w, L0_ffn_w1, L0_ffn_w2t)
    return x

_drawn_inputs = setup_inputs


def setup_inputs(seed=0):
    import zlib

    import numpy as np

    out = dict(_drawn_inputs(seed))
    spreads = {}
    factors = {'fside_Bx32xSxS2_0': 8.0}
    for name, (base, spread) in spreads.items():
        noise = np.random.default_rng([zlib.crc32(name.encode()), seed]).standard_normal(out[name].shape)
        drawn = base * np.exp(spread * noise) if base else spread * noise
        out[name] = jnp.asarray(drawn.astype(out[name].dtype))
    for name, factor in factors.items():
        out[name] = (out[name] * factor).astype(out[name].dtype)
    return out
```

```python
from contextlib import ExitStack

import numpy as np

import concourse.bass as bass
from concourse import mybir

F32 = mybir.dt.float32
F32R = mybir.dt.float32r
BF16 = mybir.dt.bfloat16
U8 = mybir.dt.uint8
ALU = mybir.AluOpType
ACT = mybir.ActivationFunctionType
AX = mybir.AxisListType

B, S, D, H, DH = 32, 64, 512, 32, 128
INTER, SPARSITY, RANK = 1792, 32, 16
P = 128
PAIRS = B * S // P
HALVES = 2
PPH = PAIRS // HALVES
HTOK = PPH * P
HPG = 2
GROUPS = H // HPG
GC = HPG * DH
ITERS = HALVES * GROUPS
CH = D // P
TB = 512
NTB = HTOK // TB
OUTS = 12
HUS = 2 * OUTS // PPH
PIECE = 1024
RAW = 3
XR = 3
SCALE = float(np.float32(1.0) / np.sqrt(np.float32(DH)))
EPS = 1e-5
MASKED = -1e37
IC = INTER // P
NBLK = INTER // SPARSITY
IB = [(0, 512), (512, 512), (1024, 512), (1536, 256)]
TGRP = [(0, 4), (4, 4), (8, 4), (12, 2)]
X2R = 5
FU = 256
SLOTS = ITERS * PPH
FIRST_SLOT = -PPH


def pieces():
    out = [("ctx", c, PIECE, FIRST_SLOT - 1) for c in range(CH)]
    out += [("wk", 0, PIECE, FIRST_SLOT - 1), ("wv", 0, PIECE, FIRST_SLOT - 1)]
    for s in range(FIRST_SLOT, SLOTS):
        it, i = divmod(s, PPH)
        if i == 1 and it + 1 < ITERS:
            out.append(("wq", it + 1, PIECE, s))
        if i == 4 and it + 1 < ITERS:
            out.append(("wo", it + 1, PIECE, s))
        if i == 3 and it + 2 < ITERS:
            out.append(("wk", it + 2, PIECE, s))
        if i == 6 and it + 2 < ITERS:
            out.append(("wv", it + 2, PIECE, s))
        if s in (xn_base(1) - 2, xn_base(1) - 1):
            c = 2 * (s - xn_base(1) + 2)
            out += [("ctx", CH + c, PIECE, s), ("ctx", CH + c + 1, PIECE, s)]
        if it == ITERS - 1 and i < 7:
            out.append(("w1", i, PIECE, s))
    end = SLOTS + 3
    out += [("c1", 0, CH * P, end), ("c2", 0, PIECE, end), ("c2", 1, INTER - PIECE, end)]
    out += [("w2", n, PIECE, end) for n in range(7)]
    return out


def xn_base(half):
    return PPH * (GROUPS * half - 1)


def x_tiles():
    out = []
    for s in range(FIRST_SLOT - 1, SLOTS + 3):
        for half in range(HALVES):
            j = s - xn_base(half)
            if 0 <= j < 4:
                out += [("ln", PPH * half + 2 * j, s), ("ln", PPH * half + 2 * j + 1, s)]
            p = s - 3 - PPH * (GROUPS * (half + 1) - 1)
            if 0 <= p < PPH:
                out.append(("res", PPH * half + p, s))
    return out


def psw_uses():
    out = []
    for s in range(FIRST_SLOT, SLOTS + 2):
        if 0 <= s - 2 < SLOTS:
            out.append(("wo", s - 2))
        for half in range(HALVES):
            j = s - xn_base(half)
            if 0 <= j < 4:
                out += [("xn", PPH * half + 2 * j), ("xn", PPH * half + 2 * j + 1)]
    return out


def build(nc, x, ctx_t, bias, mask, gates, wq, wk, wv, wo, c1, c2, w1, w2, out):
    PIECES = pieces()
    piece_no = {(k, i): n for n, (k, i, _, _) in enumerate(PIECES)}
    XT = x_tiles()
    xt_no = {(k, t): n for n, (k, t, _) in enumerate(XT)}
    PSW = psw_uses()
    psw_no = {u: n for n, u in enumerate(PSW)}
    n_psw = len(PSW)
    LN_TILES = PAIRS
    x1_dram = nc.dram_tensor("x1_between_halves", [PAIRS, P, D], F32, kind="Internal").ap()

    with ExitStack() as whole:
        def sb(stack, name, shape, dt):
            return stack.enter_context(nc.sbuf_tensor(name, shape, dt))

        def sem(name):
            return whole.enter_context(nc.semaphore(name))

        bank = [whole.enter_context(nc.psum_tensor(f"bank{i}", [P, 512], F32)) for i in range(8)]

        ident = sb(whole, "ident", [P, P], F32)
        raw = [sb(whole, f"raw{i}", [P, PIECE], F32) for i in range(RAW)]
        gate_in = sb(whole, "gate_in", [P, 2], F32)
        gate = sb(whole, "gate_tanh", [P, 2], F32)
        stats = [sb(whole, f"ln_stats{i}", [P, 6], F32) for i in range(2)]
        mv = [sb(whole, f"ln_mean_var{i}", [P, 2], F32) for i in range(2)]
        veps = [sb(whole, f"ln_var_eps{i}", [P, 1], F32) for i in range(2)]
        rstd = [sb(whole, f"ln_rstd{i}", [P, 1], F32) for i in range(2)]
        minus_half = sb(whole, "minus_half", [P, 1], F32)
        xn = [sb(whole, f"xn{i}", [P, D], F32) for i in range(2)]

        with ExitStack() as st:
            xnt = [sb(st, f"xnt_{n}", [P, CH, HTOK], F32R) for n in ("hi", "lo")]
            ctxt = [sb(st, f"ctxt_{n}", [P, CH, HTOK], F32R) for n in ("hi", "lo")]
            wkvq = {k: [sb(st, f"{k}_{n}", [P, CH, GC], F32R) for n in ("hi", "lo")]
                    for k in ("wk", "wv", "wq")}
            qt = sb(st, "qt", [P, HPG, HTOK], F32)
            kt = [sb(st, f"kt{i}", [P, HPG, HTOK], F32) for i in range(2)]
            v = [sb(st, f"v{i}", [P, PPH, GC], F32) for i in range(2)]
            acc = sb(st, "attn_sum", [P, PPH, D], F32)
            wo_s = [[sb(st, f"wo{i}_{n}", [P, HPG, D], F32R) for n in ("hi", "lo")] for i in range(2)]
            cxo = [[sb(st, f"attn_t{i}_{n}", [P, HPG, P], F32R) for n in ("hi", "lo")] for i in range(2)]
            bias_in = [sb(st, f"bias_in{i}", [P, PPH, HPG * S], F32) for i in range(2)]
            mask_in = sb(st, "mask_in", [P, PAIRS, S], U8)
            mask_add = sb(st, "mask_add", [P, PAIRS, S], BF16)
            valid = sb(st, "row_has_key", [P, PAIRS], F32)
            bm = [sb(st, f"bias_mask{i}", [P, HPG, S], F32) for i in range(2)]
            sc = [sb(st, f"scores{i}", [P, HPG, S], F32) for i in range(2)]
            ex = [sb(st, f"exp{i}", [P, HPG, S], F32) for i in range(2)]
            negmax = [sb(st, f"negmax{i}", [P, HPG], F32) for i in range(2)]
            rsum = [sb(st, f"rowsum{i}", [P, HPG], F32) for i in range(2)]
            rinv = [sb(st, f"rowinv{i}", [P, HPG], F32) for i in range(2)]
            pb = [sb(st, f"probs_blockdiag{i}", [P, HPG, P], F32) for i in range(2)]
            pt = [sb(st, f"probs_t{i}", [P, HPG, P], F32) for i in range(2)]
            xt = [sb(st, f"x_tile{i}", [P, D], F32) for i in range(XR)]

        with ExitStack() as st:
            w1s = [sb(st, f"w1_{n}", [P, CH * INTER], F32R) for n in ("hi", "lo")]
            w2s = sb(st, "w2_hi_lo_by_piece", [P, 7, 2, PIECE], F32R)
            c1s = [sb(st, f"c1_{n}", [P, CH, P], F32R) for n in ("hi", "lo")]
            c2s = sb(st, "c2_stacked", [P, INTER], F32R)
            xft = [[sb(st, f"xft{i}_{n}", [P, CH, FU], F32R) for n in ("hi", "lo")] for i in range(2)]
            ts = [sb(st, f"low_rank_stacked{i}", [P, FU], F32R) for i in range(2)]
            pick = sb(st, "selector", [P, INTER], F32)
            is_max = sb(st, "is_max", [P, NBLK, SPARSITY], BF16)
            first = [sb(st, f"first_max{i}", [P, NBLK, SPARSITY], BF16) for i in range(2)]
            m1 = sb(st, "block_max", [P, NBLK], F32)
            m2 = sb(st, "block_first", [P, NBLK], BF16)
            hm = sb(st, "h_picked", [P, INTER], F32)
            hmt = [sb(st, f"h_picked_t_{n}", [P, IC, P], F32R) for n in ("hi", "lo")]
            x2 = [sb(st, f"x1_tile{i}", [P, D], F32) for i in range(X2R)]
            rank_w = sb(st, "earlier_is_larger", [P, SPARSITY], BF16)

        raw_in = [sem(f"dma_raw{i}") for i in range(RAW)]
        bias_sem = [sem(f"dma_bias{i}") for i in range(2)]
        xt_in = [sem(f"dma_x{i}") for i in range(XR)]
        x2_in = [sem(f"dma_x1_{i}") for i in range(X2R)]
        mask_sem = sem("dma_mask")
        gate_sem = sem("dma_gate")
        x1_out = [sem(f"dma_x1_store{i}") for i in range(PPH)]
        out_sem = [sem(f"dma_out{i}") for i in range(X2R)]
        pe_proj = sem("pe_proj")
        pe_score = sem("pe_score")
        pe_pt = sem("pe_pt")
        pe_pv = sem("pe_pv")
        pe_psw = sem("pe_psw")
        act_proj = sem("act_proj")
        act_exp = sem("act_exp")
        act_pt = sem("act_pt")
        act_chi = sem("act_chi")
        act_xhi = sem("act_xhi")
        act_gate = sem("act_gate")
        dve_hi = sem("dve_hi")
        dve_s = sem("dve_s")
        dve_max = sem("dve_max")
        dve_p = sem("dve_p")
        dve_clo = sem("dve_clo")
        dve_psw = sem("dve_psw")
        dve_acc = sem("dve_acc")
        dve_stat = sem("dve_stat")
        dve_xn = sem("dve_xn")
        dve_step = sem("dve_step")
        dve_mask = sem("dve_mask")
        pool_c = sem("pool_const")
        pool_own = sem("pool_own")
        pool_bm = sem("pool_bm")
        pool_rstd = sem("pool_rstd")
        pool_lo = sem("pool_lo")
        pe_x = sem("pe_ffn_xt")
        pe_t = sem("pe_ffn_t")
        pe_i = sem("pe_ffn_inter")
        pe_h = sem("pe_ffn_h")
        pe_ht = sem("pe_ffn_ht")
        pe_o = sem("pe_ffn_out")
        act_i = sem("act_ffn_inter")
        act_h = sem("act_ffn_ht_hi")
        act_fx = sem("act_ffn_xt_hi")
        dve_fx = sem("dve_ffn_xt_lo")
        dve_t = sem("dve_ffn_t")
        dve_e = sem("dve_ffn_ismax")
        pool_e = sem("pool_ffn_rank")
        dve_oh = sem("dve_ffn_first")
        dve_hm = sem("dve_ffn_hm")
        dve_hl = sem("dve_ffn_ht_lo")
        dve_o = sem("dve_ffn_out")

        block = whole.enter_context(nc.Block())

        def wait(eng, s, n):
            if n > 0:
                eng.wait_ge(s, n)

        def ring(eng, sems, n):
            eng.wait_ge(sems[n % len(sems)], 16 * (n // len(sems) + 1))

        def dest(kind, i):
            if kind == "ctx":
                return ctxt[0][:, i % CH, :], ctxt[1][:, i % CH, :]
            if kind in wkvq:
                return [t[:, :, :].rearrange("p a b -> p (a b)") for t in wkvq[kind]]
            if kind == "wo":
                return [t[:, :, :].rearrange("p a b -> p (a b)") for t in wo_s[i % 2]]
            if kind == "w1":
                return [t[:, i * PIECE:(i + 1) * PIECE] for t in w1s]
            if kind == "w2":
                return w2s[:, i, 0, :], w2s[:, i, 1, :]
            if kind == "c1":
                return [t[:, :, :].rearrange("p a b -> p (a b)") for t in c1s]
            a = i * PIECE
            b = min(a + PIECE, INTER)
            return c2s[:, a:b], c2s[:, a:b]

        def source(kind, i):
            if kind == "ctx":
                return ctx_t[i // CH, i % CH]
            if kind in ("wk", "wv", "wq", "wo"):
                return {"wk": wk, "wv": wv, "wq": wq, "wo": wo}[kind][i % GROUPS]
            if kind == "c1":
                return c1
            t = {"w1": w1, "w2": w2, "c2": c2}[kind]
            return t[:, i * PIECE:min((i + 1) * PIECE, t.shape[1])]

        def wait_dest_free(eng, kind, i):
            if kind == "ctx" and i >= CH:
                wait(eng, pe_proj, OUTS * (GROUPS - 1) + 8)
            if kind in wkvq:
                wait(eng, pe_proj, OUTS * (i - 1) + {"wk": 4, "wv": 8, "wq": 12}[kind])
            if kind == "wo" and i >= 2:
                wait(eng, pe_psw, psw_no[("wo", PPH * (i - 1) - 1)] + 1)
            if kind == "w1":
                wait(eng, pe_proj, OUTS * ITERS)
            if kind in ("w2", "c1", "c2"):
                wait(eng, pe_proj, OUTS * ITERS)
                wait(eng, pe_score, SLOTS)
                wait(eng, pe_pv, SLOTS)

        ps_t_uses = [("x", 0), ("x", 1)]
        for j in range(PAIRS):
            if j % 2 == 0 and j + 3 < PAIRS:
                ps_t_uses += [("x", j + 2), ("x", j + 3)]
            ps_t_uses += [("h", j, k) for k in range(4)]
        ps_t_no = {u: n for n, u in enumerate(ps_t_uses)}

        def psT(use):
            return 4 + ps_t_no[use] % 2

        @block.sync
        def _(sp):
            todo = []

            def add(slot, order, f):
                todo.append((slot, order, len(todo), f))

            def load_piece(n):
                kind, i, cols, _ = PIECES[n]
                wait(sp, pool_lo, n - RAW + 1)
                sp.dma_start(raw[n % RAW][:, 0:cols], source(kind, i)).then_inc(raw_in[n % RAW], 16)

            def load_x(n):
                kind, t, _ = XT[n]
                if n >= XR:
                    k0, t0, _ = XT[n - XR]
                    if k0 == "ln":
                        wait(sp, dve_xn, t0 + 1)
                    else:
                        wait(sp, dve_acc, t0 + 1)
                sp.dma_start(xt[n % XR][:, :], x[t]).then_inc(xt_in[n % XR], 16)

            def load_bias(it):
                wait(sp, pool_bm, PPH * (it - 1))
                sp.dma_start(bias_in[it % 2][:, :, :], bias[it]).then_inc(bias_sem[it % 2], 16)

            def store_x1(t):
                wait(sp, dve_acc, t + 1)
                sp.dma_start(x1_dram[t], acc[:, t % PPH, :]).then_inc(x1_out[t % PPH], 16)

            sp.dma_start(gate_in[:, :], gates).then_inc(gate_sem, 16)
            sp.dma_start(mask_in[:, :, :], mask).then_inc(mask_sem, 16)
            for n in range(len(PIECES)):
                add(PIECES[n - RAW][3] if n >= RAW else -99, 0, lambda n=n: load_piece(n))
            for n in range(len(XT)):
                add(XT[n - XR][2] if n >= XR else -98, 1, lambda n=n: load_x(n))
            for it in range(ITERS):
                add(PPH * (it - 1), 2, lambda it=it: load_bias(it))
            for t in range(PAIRS):
                it = GROUPS * (t // PPH + 1) - 1
                add(PPH * it + t % PPH + 4, 3, lambda t=t: store_x1(t))
            for item in sorted(todo, key=lambda a: a[:3]):
                item[3]()
            def load_x2(t):
                if t >= X2R:
                    sp.wait_ge(out_sem[t % X2R], 16 * (t // X2R))
                else:
                    wait(sp, dve_acc, PAIRS)
                    wait(sp, pool_bm, SLOTS)
                    wait(sp, pe_psw, n_psw)
                sp.wait_ge(x1_out[t % PPH], 16 * (t // PPH + 1))
                sp.dma_start(x2[t % X2R][:, :], x1_dram[t]).then_inc(x2_in[t % X2R], 16)

            for t in range(X2R):
                load_x2(t)
            for t in range(PAIRS):
                wait(sp, dve_o, t + 1)
                sp.dma_start(out[t], x2[t % X2R][:, :]).then_inc(out_sem[t % X2R], 16)
                if t + X2R < PAIRS:
                    load_x2(t + X2R)
            for k in range(X2R):
                sp.wait_ge(out_sem[k], 16 * len(range(k, PAIRS, X2R)))
            for k in range(PPH):
                sp.wait_ge(x1_out[k], 16 * HALVES)

        @block.gpsimd
        def _(pool):
            pool.memset(ident[:, :], 0.0).then_inc(pool_own, 1)
            for i in range(2):
                pool.memset(pb[i][:, :, :], 0.0).then_inc(pool_c, 1)
            pool.memset(minus_half[:, :], -0.5).then_inc(pool_c, 1)
            wait(pool, pool_own, 1)
            pool.affine_select(out=ident[:, :], in_=ident[:, :], compare_op=ALU.not_equal, fill=1.0,
                               base=0, pattern=[[-1, P]], channel_multiplier=1).then_inc(pool_c, 1)
            own = [1]

            def do_rstd(n):
                wait(pool, dve_stat, n + 1)
                wait(pool, dve_xn, n - 1)
                pool.tensor_scalar(veps[n % 2][:, :], mv[n % 2][:, 1:2], EPS, None, ALU.add)\
                    .then_inc(pool_own, 1)
                own[0] += 1
                wait(pool, pool_own, own[0])
                pool.tensor_tensor(rstd[n % 2][:, :], veps[n % 2][:, :], minus_half[:, :], ALU.pow)\
                    .then_inc(pool_rstd, 1)

            def do_bm(s):
                it, p = divmod(s, PPH)
                if p == 0:
                    ring(pool, bias_sem, it)
                wait(pool, dve_s, s - 1)
                tile = PPH * (it // GROUPS) + p
                pool.tensor_tensor(
                    bm[s % 2][:, :, :], bias_in[it % 2][:, p, :].rearrange("p (h k) -> p h k", h=HPG),
                    mask_add[:, tile, :].unsqueeze(1).broadcast_to([P, HPG, S]), ALU.add)\
                    .then_inc(pool_bm, 1)

            def do_lo(n):
                kind, i, cols, _ = PIECES[n]
                hi, lo = dest(kind, i)
                wait(pool, dve_hi, n + 1)
                r = raw[n % RAW]
                if kind != "c2":
                    if kind == "w2" and i == 0:
                        wait(pool, pool_lo, n)
                    pool.tensor_tensor(lo, r[:, 0:cols], hi.bitcast(F32), ALU.subtract)\
                        .then_inc(pool_lo, 1)
                    return
                for q in (32, 96):
                    wait(pool, pool_lo, n)
                    wait(pool, pool_own, own[0])
                    last = pool.tensor_tensor(lo[q:q + 32], r[q:q + 32, 0:cols],
                                              hi[q:q + 32].bitcast(F32), ALU.subtract)
                    if q == 32:
                        last.then_inc(pool_own, 1)
                        own[0] += 1
                last.then_inc(pool_lo, 1)

            wait(pool, pool_c, 4)
            wait(pool, dve_mask, 2)
            n = 0
            for s in range(FIRST_SLOT - 1, SLOTS + 4):
                for k, t, slot in XT:
                    if k == "ln" and slot == s:
                        do_rstd(t)
                if 0 <= s + 1 < SLOTS:
                    do_bm(s + 1)
                while n < len(PIECES) and PIECES[n][3] == s:
                    do_lo(n)
                    n += 1
            for t in range(SPARSITY):
                last = pool.memset(rank_w[:, t:t + 1], float(SPARSITY - t))
            last.then_inc(pool_own, 1)
            own[0] += 1
            wait(pool, pool_own, own[0])
            do_rstd(LN_TILES)
            do_rstd(LN_TILES + 1)

            def rank(t):
                wait(pool, dve_e, t + 1)
                pool.tensor_tensor(is_max[:, :, :], is_max[:, :, :],
                                   rank_w[:, :].unsqueeze(1).broadcast_to([P, NBLK, SPARSITY]), ALU.mult)\
                    .then_inc(pool_e, 1)

            rank(0)
            for j in range(PAIRS):
                if j % 2 == 0 and j + 3 < PAIRS:
                    do_rstd(LN_TILES + j + 2)
                    do_rstd(LN_TILES + j + 3)
                if j + 1 < PAIRS:
                    rank(j + 1)

        @block.scalar
        def _(act):
            act.wait_ge(gate_sem, 16)
            act.activation(gate[:, :], gate_in[:, :], ACT.Tanh).then_inc(act_gate, 1)

            def evac(n):
                it, k = divmod(n, OUTS)
                wait(act, pe_proj, n + 1)
                b = bank[n % 2][:, :]
                if k < 4:
                    tb, h = divmod(k, HPG)
                    wait(act, pe_score, PPH * (it - 1))
                    o = kt[it % 2][:, h, tb * TB:(tb + 1) * TB]
                elif k < 8:
                    j = k - 4
                    wait(act, pe_pv, PPH * (it - 1))
                    o = v[it % 2][:, 2 * j:2 * j + 2, :].rearrange("p a b -> p (a b)")
                else:
                    tb, h = divmod(k - 8, HPG)
                    wait(act, pe_score, PPH * (it - 1) + (tb + 1) * (TB // P))
                    o = qt[:, h, tb * TB:(tb + 1) * TB]
                act.activation(o, b, ACT.Copy).then_inc(act_proj, 1)

            def exps(s):
                wait(act, dve_max, s + 1)
                wait(act, dve_p, s - 1)
                for h in range(HPG):
                    last = act.activation(ex[s % 2][:, h, :], sc[s % 2][:, h, :], ACT.Exp,
                                          bias=negmax[s % 2][:, h:h + 1], scale=1.0,
                                          accum_out=rsum[s % 2][:, h:h + 1])
                last.then_inc(act_exp, 1)

            def probs_t(s):
                wait(act, pe_pt, s + 1)
                wait(act, pe_pv, s - 1)
                act.activation(pt[s % 2][:, :, :].rearrange("p a b -> p (a b)"), bank[4][:, 0:HPG * P],
                               ACT.Copy).then_inc(act_pt, 1)

            def chi(s):
                wait(act, pe_pv, s + 1)
                if s >= 2:
                    wait(act, pe_psw, psw_no[("wo", s - 2)] + 1)
                act.activation(cxo[s % 2][0][:, :, :].rearrange("p a b -> p (a b)"),
                               bank[5][:, 0:HPG * P], ACT.Copy).then_inc(act_chi, 1)

            def xhi(t):
                n = psw_no[("xn", t)]
                wait(act, pe_psw, n + 1)
                if t >= PPH:
                    wait(act, pe_proj, OUTS * GROUPS)
                p = t % PPH
                act.activation(xnt[0][:, :, p * P:(p + 1) * P],
                               bank[6 + n % 2][:, :].rearrange("p (c t) -> p c t", c=CH),
                               ACT.Copy).then_inc(act_xhi, 1)

            for s in range(FIRST_SLOT, SLOTS + 2):
                it, i = divmod(s, PPH)
                done = []
                if it + 1 < ITERS:
                    done = [OUTS * (it + 1) + (HUS * i + u) // 2 if (HUS * i + u) % 2 else None
                            for u in range(HUS)]
                for half in range(HALVES):
                    j = s - 1 - xn_base(half)
                    if 0 <= j < 4:
                        xhi(PPH * half + 2 * j)
                        xhi(PPH * half + 2 * j + 1)
                if done and done[0] is not None:
                    evac(done[0])
                if 0 <= s - 1 < SLOTS:
                    probs_t(s - 1)
                if 0 <= s < SLOTS:
                    exps(s)
                if done and done[1] is not None:
                    evac(done[1])
                if 0 <= s - 1 < SLOTS:
                    chi(s - 1)
                if done and done[2] is not None:
                    evac(done[2])

            def fx_hi(t):
                wait(act, pe_x, t + 1)
                wait(act, pe_h, 4 * (2 * (t // 2) - 2))
                u, a = divmod(t, 2)
                act.activation(xft[u % 2][0][:, :, a * P:(a + 1) * P],
                               bank[psT(("x", t))][:, :].rearrange("p (c t) -> p c t", c=CH),
                               ACT.Copy).then_inc(act_fx, 1)

            def sel(t):
                wait(act, dve_e, t)
                for k, (a, w) in enumerate(IB):
                    wait(act, pe_i, 4 * t + k + 1)
                    act.activation(pick[:, a:a + w], bank[2 + k % 2][:, 0:w], ACT.Copy).then_inc(act_i, 1)

            def ht_hi(t, k):
                a, w = TGRP[k]
                wait(act, pe_ht, 4 * t + k + 1)
                act.activation(hmt[0][:, a:a + w, :].rearrange("p a b -> p (a b)"),
                               bank[psT(("h", t, k))][:, 0:w * P], ACT.Copy).then_inc(act_h, 1)

            wait(act, pool_lo, len(PIECES))
            wait(act, pe_psw, n_psw)
            wait(act, dve_acc, PAIRS)
            fx_hi(0)
            fx_hi(1)
            sel(0)
            for j in range(PAIRS):
                if j + 1 < PAIRS:
                    sel(j + 1)
                if j % 2 == 0 and j + 3 < PAIRS:
                    fx_hi(j + 2)
                    fx_hi(j + 3)
                for k in range(4):
                    ht_hi(j, k)

        @block.vector
        def _(dve):
            step = [0]

            def link(ins):
                step[0] += 1
                ins.then_inc(dve_step, 1)
                return step[0]

            def after(n):
                dve.wait_ge(dve_step, n)

            dve.wait_ge(mask_sem, 16)
            dve.tensor_scalar(mask_add[:, :, :], mask_in[:, :, :], -MASKED, MASKED, ALU.mult, ALU.add)\
                .then_inc(dve_mask, 1)
            dve.tensor_reduce(valid[:, :], mask_in[:, :, :], AX.X, ALU.max).then_inc(dve_mask, 1)

            def do_hi(n):
                kind, i, cols, _ = PIECES[n]
                hi, _ = dest(kind, i)
                wait_dest_free(dve, kind, i)
                ring(dve, raw_in, n)
                dve.tensor_copy(hi, raw[n % RAW][:, 0:cols]).then_inc(dve_hi, 1)

            def ln_stats(n, src):
                wait(dve, dve_xn, n - 1)
                wait(dve, pool_rstd, n - 1)
                a = link(dve.bn_stats(stats[n % 2][:, :], src))
                after(a)
                dve.bn_aggr(mv[n % 2][:, :], stats[n % 2][:, :]).then_inc(dve_stat, 1)

            def ln_norm(n, src, transposed, k):
                wait(dve, pool_rstd, n + 1)
                wait(dve, transposed, k)
                dve.tensor_scalar(xn[n % 2][:, :], src, mv[n % 2][:, 0:1], rstd[n % 2][:, :],
                                  ALU.subtract, ALU.mult).then_inc(dve_xn, 1)

            def scores(s):
                wait(dve, pe_score, s + 1)
                wait(dve, pool_bm, s + 1)
                wait(dve, act_exp, s - 1)
                dve.scalar_tensor_tensor(out=sc[s % 2][:, :, :],
                                         in0=bank[2 + s % 2][:, 0:HPG * S].rearrange("p (h k) -> p h k", h=HPG),
                                         scalar=SCALE, in1=bm[s % 2][:, :, :],
                                         op0=ALU.mult, op1=ALU.add).then_inc(dve_s, 1)
                wait(dve, dve_s, s + 1)
                dve.tensor_reduce(negmax[s % 2][:, :], sc[s % 2][:, :, :], AX.X, ALU.max, negate=True)\
                    .then_inc(dve_max, 1)

            def probs(s):
                tile = PPH * (s // PPH // GROUPS) + s % PPH
                wait(dve, act_exp, s + 1)
                a = link(dve.reciprocal(rinv[s % 2][:, :], rsum[s % 2][:, :]))
                after(a)
                wait(dve, pe_pt, s - 1)
                for q in range(2):
                    r = slice(q * S, (q + 1) * S)
                    last = dve.scalar_tensor_tensor(
                        out=pb[s % 2][r, :, q * S:(q + 1) * S], in0=ex[s % 2][r, :, :],
                        scalar=valid[r, tile:tile + 1],
                        in1=rinv[s % 2][r, :].unsqueeze(2).broadcast_to([S, HPG, S]),
                        op0=ALU.mult, op1=ALU.mult)
                last.then_inc(dve_p, 1)

            def clo(s):
                wait(dve, act_chi, s + 1)
                hi, lo = (t[:, :, :].rearrange("p a b -> p (a b)") for t in cxo[s % 2])
                dve.tensor_tensor(lo, bank[5][:, 0:HPG * P], hi.bitcast(F32), ALU.subtract)\
                    .then_inc(dve_clo, 1)

            def add_wo(s):
                it, p = divmod(s, PPH)
                tile = PPH * (it // GROUPS) + p
                n = psw_no[("wo", s)]
                wait(dve, pe_psw, n + 1)
                b = bank[6 + n % 2][:, :]
                if it % GROUPS == 0:
                    if it:
                        dve.wait_ge(x1_out[p], 16)
                    dve.tensor_copy(acc[:, p, :], b).then_inc(dve_psw, 1)
                    return
                dve.tensor_tensor(acc[:, p, :], acc[:, p, :], b, ALU.add).then_inc(dve_psw, 1)
                if it % GROUPS == GROUPS - 1:
                    m = xt_no[("res", tile)]
                    ring(dve, xt_in, m)
                    wait(dve, dve_psw, n + 1)
                    dve.scalar_tensor_tensor(out=acc[:, p, :], in0=acc[:, p, :], scalar=gate[:, 0:1],
                                             in1=xt[m % XR][:, :], op0=ALU.mult, op1=ALU.add)\
                        .then_inc(dve_acc, 1)

            def xlo(t):
                n = psw_no[("xn", t)]
                p = t % PPH
                wait(dve, act_xhi, t + 1)
                dve.tensor_tensor(xnt[1][:, :, p * P:(p + 1) * P],
                                  bank[6 + n % 2][:, :].rearrange("p (c t) -> p c t", c=CH),
                                  xnt[0][:, :, p * P:(p + 1) * P].bitcast(F32), ALU.subtract)\
                    .then_inc(dve_psw, 1)

            wait(dve, pool_c, 4)
            wait(dve, act_gate, 1)
            n = 0
            for s in range(FIRST_SLOT - 1, SLOTS + 4):
                before = [PPH * half + 2 * (s - 1 - xn_base(half)) for half in range(HALVES)
                          if 0 <= s - 1 - xn_base(half) < 4]
                if before:
                    if 0 <= s - 3 < SLOTS:
                        add_wo(s - 3)
                    xlo(before[0])
                    xlo(before[0] + 1)
                if 0 <= s < SLOTS:
                    scores(s)
                if 0 <= s - 3 < SLOTS and not before:
                    add_wo(s - 3)
                for k, t, slot in XT:
                    if k == "ln" and slot == s:
                        m = xt_no[("ln", t)]
                        ring(dve, xt_in, m)
                        ln_stats(t, xt[m % XR][:, :])
                        ln_norm(t, xt[m % XR][:, :], pe_psw,
                                psw_no[("xn", t - 2)] + 1 if t >= 2 else 0)
                if 0 <= s < SLOTS:
                    probs(s)
                while n < len(PIECES) and PIECES[n][3] == s:
                    do_hi(n)
                    n += 1
                if 0 <= s - 1 < SLOTS:
                    clo(s - 1)

            L = LN_TILES

            def f_ln(t):
                ring(dve, x2_in, t)
                ln_stats(L + t, x2[t % X2R][:, :])
                if t >= 2:
                    ln_norm(L + t, x2[t % X2R][:, :], pe_x, t - 1)
                else:
                    ln_norm(L + t, x2[t % X2R][:, :], pe_psw, n_psw)

            def fx_lo(t):
                u, a = divmod(t, 2)
                wait(dve, act_fx, t + 1)
                dve.tensor_tensor(xft[u % 2][1][:, :, a * P:(a + 1) * P],
                                  bank[psT(("x", t))][:, :].rearrange("p (c t) -> p c t", c=CH),
                                  xft[u % 2][0][:, :, a * P:(a + 1) * P].bitcast(F32), ALU.subtract)\
                    .then_inc(dve_fx, 1)

            def low_rank(u):
                wait(dve, pe_t, u + 1)
                wait(dve, pe_i, 4 * 2 * (u - 1))
                a = link(dve.tensor_copy(ts[u % 2][:, :], bank[7][:, 0:FU]))
                after(a)
                dve.tensor_tensor(ts[u % 2][64:128, :], bank[7][64:128, 0:FU],
                                  ts[u % 2][64:128, :].bitcast(F32), ALU.subtract).then_inc(dve_t, 1)

            blk = pick[:, :].rearrange("p (n k) -> p n k", k=SPARSITY)
            mx_done = [0]

            def block_max(t, ks):
                for k in ks:
                    a, w = IB[k]
                    wait(dve, act_i, 4 * t + k + 1)
                    mx_done[0] = link(dve.tensor_reduce(
                        m1[:, a // SPARSITY:(a + w) // SPARSITY],
                        blk[:, a // SPARSITY:(a + w) // SPARSITY, :], AX.X, ALU.max))

            def mark_max(t):
                after(mx_done[0])
                dve.tensor_tensor(is_max[:, :, :], blk, m1[:, :].unsqueeze(2).broadcast_to([P, NBLK, SPARSITY]),
                                  ALU.is_equal).then_inc(dve_e, 1)

            def first_max(t):
                wait(dve, pool_e, t + 1)
                a = link(dve.tensor_reduce(m2[:, :], is_max[:, :, :], AX.X, ALU.max))
                after(a)
                wait(dve, dve_hm, 4 * (t - 1))
                dve.tensor_tensor(first[t % 2][:, :, :], is_max[:, :, :],
                                  m2[:, :].unsqueeze(2).broadcast_to([P, NBLK, SPARSITY]),
                                  ALU.is_equal).then_inc(dve_oh, 1)

            def pick_h(t, k):
                a, w = IB[k]
                wait(dve, pe_h, 4 * t + k + 1)
                wait(dve, dve_oh, t + 1)
                wait(dve, pe_ht, 4 * (t - 1) + 4)
                dve.scalar_tensor_tensor(
                    out=hm[:, a:a + w], in0=bank[k % 2][:, 0:w], scalar=0.0,
                    in1=first[t % 2][:, :, :].rearrange("p a b -> p (a b)")[:, a:a + w],
                    op0=ALU.max, op1=ALU.mult).then_inc(dve_hm, 1)

            def ht_lo(t, k):
                a, w = TGRP[k]
                wait(dve, act_h, 4 * t + k + 1)
                hi, lo = (x[:, a:a + w, :].rearrange("p a b -> p (a b)") for x in hmt)
                dve.tensor_tensor(lo, bank[psT(("h", t, k))][:, 0:w * P], hi.bitcast(F32), ALU.subtract)\
                    .then_inc(dve_hl, 1)

            def finish(t):
                wait(dve, pe_o, t + 1)
                dve.scalar_tensor_tensor(out=x2[t % X2R][:, :], in0=bank[6][:, :], scalar=gate[:, 1:2],
                                         in1=x2[t % X2R][:, :], op0=ALU.mult, op1=ALU.add)\
                    .then_inc(dve_o, 1)

            f_ln(0)
            f_ln(1)
            fx_lo(0)
            fx_lo(1)
            low_rank(0)
            block_max(0, range(4))
            mark_max(0)
            first_max(0)
            for j in range(PAIRS):
                nxt = j + 1 < PAIRS
                if nxt:
                    block_max(j + 1, (0, 1))
                pick_h(j, 0)
                if nxt:
                    block_max(j + 1, (2, 3))
                pick_h(j, 1)
                prep = j % 2 == 0 and j + 3 < PAIRS
                if prep:
                    f_ln(j + 2)
                    f_ln(j + 3)
                pick_h(j, 2)
                if nxt:
                    mark_max(j + 1)
                pick_h(j, 3)
                if prep:
                    fx_lo(j + 2)
                    fx_lo(j + 3)
                if nxt:
                    first_max(j + 1)
                for k in range(3):
                    ht_lo(j, k)
                if prep:
                    low_rank(j // 2 + 1)
                if j:
                    finish(j - 1)
                ht_lo(j, 3)
            finish(PAIRS - 1)

        @block.tensor
        def _(pe):
            def three(o, a, b, first_mm, last_mm):
                pe.matmul(o, a[0], b[0], start=first_mm, stop=False)
                pe.matmul(o, a[0], b[1], start=False, stop=False)
                return pe.matmul(o, a[1], b[0], start=False, stop=last_mm)

            def hi_lo(ts_, *idx):
                return [t[idx] for t in ts_]

            full = slice(None)

            def half_output(it, u):
                k, second = divmod(u, 2)
                n = OUTS * it + k
                b = bank[n % 2]
                if not second:
                    wait(pe, act_proj, n - 1)
                    if k % 4 == 0:
                        kind = ("wk", "wv", "wq")[k // 4]
                        wait(pe, pool_lo, piece_no[(kind, it)] + 1)
                        if k == 0 and it % GROUPS == 0:
                            wait(pe, pool_lo, piece_no[("ctx", CH * (it // GROUPS) + CH - 1)] + 1)
                        if k == 8 and it % GROUPS == 0:
                            wait(pe, dve_psw, psw_no[("xn", PPH * (it // GROUPS) + PPH - 1)] + 1)
                if 4 <= k < 8:
                    tile = 2 * (k - 4) + second
                    o = b[:, second * GC:(second + 1) * GC]
                    for c in range(CH):
                        mm = three(o, hi_lo(ctxt, full, c, slice(tile * P, (tile + 1) * P)),
                                   hi_lo(wkvq["wv"], full, c, full), c == 0, c == CH - 1)
                else:
                    w, xx = (wkvq["wk"], ctxt) if k < 4 else (wkvq["wq"], xnt)
                    tb, h = divmod(k % 4, HPG)
                    for c in (2 * second, 2 * second + 1):
                        mm = three(b[:, :], hi_lo(w, full, c, slice(h * DH, (h + 1) * DH)),
                                   hi_lo(xx, full, c, slice(tb * TB, (tb + 1) * TB)),
                                   c == 0, c == CH - 1)
                if second:
                    mm.then_inc(pe_proj, 1)

            def scores(s):
                it, p = divmod(s, PPH)
                if p == 0:
                    wait(pe, act_proj, OUTS * (it + 1))
                wait(pe, dve_s, s - 1)
                for q in range(2):
                    cols = slice(p * P + q * S, p * P + (q + 1) * S)
                    for h in range(HPG):
                        mm = pe.matmul(bank[2 + s % 2][q * S:(q + 1) * S, h * S:(h + 1) * S],
                                       qt[:, h, cols], kt[it % 2][:, h, cols], start=True, stop=True)
                mm.then_inc(pe_score, 1)

            def probs_t(s):
                wait(pe, dve_p, s + 1)
                wait(pe, act_pt, s)
                for h in range(HPG):
                    mm = pe.transpose(bank[4][:, h * P:(h + 1) * P], pb[s % 2][:, h, :], ident[:, :])
                mm.then_inc(pe_pt, 1)

            def attend(s):
                it, p = divmod(s, PPH)
                wait(pe, act_pt, s + 1)
                wait(pe, dve_clo, s)
                for h in range(HPG):
                    mm = pe.matmul(bank[5][:, h * P:(h + 1) * P], v[it % 2][:, p, h * DH:(h + 1) * DH],
                                   pt[s % 2][:, h, :], start=True, stop=True)
                mm.then_inc(pe_pv, 1)

            def project_out(s):
                it = s // PPH
                n = psw_no[("wo", s)]
                wait(pe, dve_psw, n - 1)
                if s % PPH == 0:
                    wait(pe, pool_lo, piece_no[("wo", it)] + 1)
                wait(pe, dve_clo, s + 1)
                for h in range(HPG):
                    mm = three(bank[6 + n % 2][:, :], hi_lo(cxo[s % 2], full, h, full),
                               hi_lo(wo_s[it % 2], full, h, full), h == 0, h == HPG - 1)
                mm.then_inc(pe_psw, 1)

            def transpose_x(t):
                n = psw_no[("xn", t)]
                wait(pe, dve_psw, n - 1)
                wait(pe, dve_xn, t + 1)
                for c in range(CH):
                    mm = pe.transpose(bank[6 + n % 2][:, c * P:(c + 1) * P], xn[t % 2][:, c * P:(c + 1) * P],
                                      ident[:, :])
                mm.then_inc(pe_psw, 1)

            wait(pe, pool_c, 4)
            for s in range(FIRST_SLOT, SLOTS + 2):
                it, i = divmod(s, PPH)
                unit = (lambda u: half_output(it + 1, HUS * i + u)) if it + 1 < ITERS else (lambda u: None)
                if 0 <= s < SLOTS:
                    scores(s)
                unit(0)
                if 0 <= s - 1 < SLOTS:
                    probs_t(s - 1)
                unit(1)
                if 0 <= s - 1 < SLOTS:
                    attend(s - 1)
                unit(2)
                if 0 <= s - 2 < SLOTS:
                    project_out(s - 2)
                for half in range(HALVES):
                    j = s - xn_base(half)
                    if 0 <= j < 4:
                        transpose_x(PPH * half + 2 * j)
                        transpose_x(PPH * half + 2 * j + 1)

            wait(pe, act_chi, SLOTS)
            wait(pe, dve_clo, SLOTS)
            wait(pe, dve_psw, n_psw)
            wait(pe, act_proj, OUTS * ITERS)

            def f_bank_free(use):
                n = ps_t_no[use] - 2
                if n < 0:
                    return
                u = ps_t_uses[n]
                if u[0] == "x":
                    wait(pe, dve_fx, u[1] + 1)
                else:
                    wait(pe, dve_hl, 4 * u[1] + u[2] + 1)

            def f_transpose_x(t):
                f_bank_free(("x", t))
                wait(pe, dve_xn, LN_TILES + t + 1)
                for c in range(CH):
                    mm = pe.transpose(bank[psT(("x", t))][:, c * P:(c + 1) * P],
                                      xn[t % 2][:, c * P:(c + 1) * P], ident[:, :])
                mm.then_inc(pe_x, 1)

            def low_rank(u):
                wait(pe, dve_fx, 2 * u + 2)
                wait(pe, dve_t, u)
                if u == 0:
                    wait(pe, pool_lo, piece_no[("c2", 1)] + 1)
                for c in range(CH):
                    mm = three(bank[7][:, 0:FU], hi_lo(c1s, full, c, full),
                               hi_lo(xft[u % 2], full, c, full), c == 0, c == CH - 1)
                mm.then_inc(pe_t, 1)

            def selector(t):
                u, a = divmod(t, 2)
                wait(pe, dve_t, u + 1)
                for k, (c0, w) in enumerate(IB):
                    wait(pe, act_i, 4 * t + k - 1)
                    pe.matmul(bank[2 + k % 2][:, 0:w], ts[u % 2][:, a * P:(a + 1) * P],
                              c2s[:, c0:c0 + w], start=True, stop=True).then_inc(pe_i, 1)

            def hidden(t):
                u, a = divmod(t, 2)
                for k, (c0, w) in enumerate(IB):
                    wait(pe, dve_hm, 4 * t + k - 1)
                    for c in range(CH):
                        mm = three(bank[k % 2][:, 0:w],
                                   hi_lo(xft[u % 2], full, c, slice(a * P, (a + 1) * P)),
                                   hi_lo(w1s, full, slice(c * INTER + c0, c * INTER + c0 + w)),
                                   c == 0, c == CH - 1)
                    mm.then_inc(pe_h, 1)

            def transpose_h(t, k):
                a, w = TGRP[k]
                f_bank_free(("h", t, k))
                wait(pe, dve_hm, 4 * t + k + 1)
                for c in range(a, a + w):
                    mm = pe.transpose(bank[psT(("h", t, k))][:, (c - a) * P:(c - a + 1) * P],
                                      hm[:, c * P:(c + 1) * P], ident[:, :])
                mm.then_inc(pe_ht, 1)

            def output(t, k):
                a, w = TGRP[k]
                wait(pe, dve_hl, 4 * t + k + 1)
                if k == 0:
                    wait(pe, dve_o, t)
                if t == 0:
                    wait(pe, pool_lo, piece_no[("w2", (a + w - 1) // 2)] + 1)
                for c in range(a, a + w):
                    o = (c % 2) * D
                    wh, wl = (w2s[:, c // 2, q, o:o + D] for q in range(2))
                    mm = three(bank[6][:, :], hi_lo(hmt, full, c, full), (wh, wl), c == 0, c == IC - 1)
                if k == 3:
                    mm.then_inc(pe_o, 1)

            f_transpose_x(0)
            f_transpose_x(1)
            low_rank(0)
            selector(0)
            wait(pe, pool_lo, piece_no[("w1", 6)] + 1)
            for j in range(PAIRS):
                if j + 1 < PAIRS:
                    selector(j + 1)
                hidden(j)
                prep = j % 2 == 0 and j + 3 < PAIRS
                if prep:
                    f_transpose_x(j + 2)
                    f_transpose_x(j + 3)
                for k in range(4):
                    if j:
                        output(j - 1, k)
                    if k == 3 and prep:
                        low_rank(j // 2 + 1)
                    transpose_h(j, k)
            for k in range(4):
                output(PAIRS - 1, k)


_ORDER = ["x", "ctx_t", "bias", "mask", "gates", "wq", "wk", "wv", "wo", "c1", "c2", "w1", "w2"]


def layouts(a):
    def cols(w):
        return w.reshape(CH, P, GROUPS, GC).transpose(2, 1, 0, 3).reshape(GROUPS, P, CH * GC)

    gates = np.concatenate([np.broadcast_to(a["g_xattn"].reshape(1, 1), (P, 1)),
                            np.broadcast_to(a["g_ffn"].reshape(1, 1), (P, 1))], axis=1)
    bias = a["fside_Bx32xSxS2_0"].reshape(HALVES, PPH, 2, GROUPS, HPG, S, S)
    bias = bias.transpose(0, 3, 2, 5, 1, 4, 6).reshape(ITERS, P, PPH, HPG * S)
    mask = a["mask_BxSxS2_bk0"].reshape(PAIRS, P, S).transpose(1, 0, 2)
    c1 = np.zeros((D, 4, 32), np.float32)
    c1[:, :, :RANK] = a["L0_ffn_c1_w"].T[:, None, :]
    c2 = np.zeros((4, 32, INTER), np.float32)
    c2[:, :RANK, :] = a["L0_ffn_c2_w"].T[None]
    return {
        "x": a["x"].reshape(PAIRS, P, D),
        "ctx_t": a["ctx_4096"].reshape(B * S, D).T.reshape(CH, P, HALVES, HTOK).transpose(2, 0, 1, 3),
        "bias": bias,
        "mask": mask,
        "gates": gates,
        "wq": cols(a["L0_xattn_Wq"]),
        "wk": cols(a["L0_xattn_Wk"]),
        "wv": cols(a["L0_xattn_Wv"]),
        "wo": a["L0_xattn_Wo"].reshape(GROUPS, HPG, P, D).transpose(0, 2, 1, 3).reshape(GROUPS, P, HPG * D),
        "c1": c1.reshape(CH, P, P).transpose(1, 0, 2).reshape(P, CH * P),
        "c2": c2.reshape(P, INTER),
        "w1": a["L0_ffn_w1"].T.reshape(CH, P, INTER).transpose(1, 0, 2).reshape(P, CH * INTER),
        "w2": a["L0_ffn_w2t"].reshape(IC, P, D).transpose(1, 0, 2).reshape(P, IC * D),
    }


def kernel(**inputs):
    import concourse.bacc as bacc
    from concourse.bass_utils import run_bass_kernel_spmd

    laid = layouts({k: np.asarray(v) for k, v in inputs.items()})
    nc = bacc.Bacc("TRN2", target_bir_lowering=False, num_devices=1)
    arrays, args = {}, []
    for name in _ORDER:
        a = np.ascontiguousarray(laid[name])
        arrays[f"in_{name}"] = a
        args.append(nc.dram_tensor(f"in_{name}", a.shape, mybir.dt.from_np(a.dtype), kind="ExternalInput").ap())
    out = nc.dram_tensor("out_0", [PAIRS, P, D], F32, kind="ExternalOutput").ap()
    build(nc, *args, out)
    r = run_bass_kernel_spmd(nc, [arrays], core_ids=[0])
    return r.results[0]["out_0"].reshape(B, S, D)
```

```python
from contextlib import ExitStack

import numpy as np

import concourse.bass as bass
from concourse import mybir

F32 = mybir.dt.float32
F32R = mybir.dt.float32r
BF16 = mybir.dt.bfloat16
U8 = mybir.dt.uint8
ALU = mybir.AluOpType
ACT = mybir.ActivationFunctionType
AX = mybir.AxisListType

B, S, D, H, DH = 32, 64, 512, 32, 128
INTER, SPARSITY, RANK = 1792, 32, 16
P = 128
PAIRS = B * S // P
HALVES = 2
PPH = PAIRS // HALVES
HTOK = PPH * P
HPG = 2
GROUPS = H // HPG
GC = HPG * DH
ITERS = HALVES * GROUPS
CH = D // P
TB = 512
NTB = HTOK // TB
OUTS = 12
HUS = 2 * OUTS // PPH
PIECE = 1024
RAW = 3
XR = 3
SCALE = float(np.float32(1.0) / np.sqrt(np.float32(DH)))
EPS = 1e-5
MASKED = -1e37
IC = INTER // P
NBLK = INTER // SPARSITY
IB = [(0, 512), (512, 512), (1024, 512), (1536, 256)]
TGRP = [(0, 4), (4, 4), (8, 4), (12, 2)]
X2R = 5
FU = 256
SLOTS = ITERS * PPH
FIRST_SLOT = -PPH
POOL_CONSTS = 4 + SPARSITY


def pieces():
    start = [("wk", 0, PIECE)] + [("ctx", c, PIECE) for c in range(CH)] + [("wv", 0, PIECE)]
    out = [(*q, FIRST_SLOT - 1, "act", "dve") for q in start]
    for s in range(FIRST_SLOT, SLOTS):
        it, i = divmod(s, PPH)
        for at, kind, nxt in ((1, "wq", 1), (4, "wo", 1), (3, "wk", 2), (6, "wv", 2)):
            if i == at and it + nxt < ITERS:
                out.append((kind, it + nxt, PIECE, s, "dve", "pool"))
        if s in (xn_base(1) - 2, xn_base(1) - 1):
            c = CH + 2 * (s - xn_base(1) + 2)
            out += [("ctx", c, PIECE, s, "dve", "dve"), ("ctx", c + 1, PIECE, s, "dve", "dve")]
        if it == ITERS - 1 and i == 0:
            out += [("c1", 0, CH * P, s, "act", "pool"), ("c2", 0, PIECE, s, "act", "dve"),
                    ("c2", 1, INTER - PIECE, s, "act", "dve")]
        if it == ITERS - 1 and i:
            out.append(("w1", i - 1, PIECE, s, "act", "dve" if i in (1, 4) else "pool"))
    out += [("w2", n, PIECE, SLOTS + 3, "act", "pool" if n % 2 else "dve") for n in range(7)]
    return out


def ffn_uses():
    turn = [0, 0]

    def two(base, i, use):
        turn[i] += 1
        return (use, base + (turn[i] - 1) % 2)

    out = [two(0, 0, ("x", 0)), two(0, 0, ("x", 1)), two(0, 0, ("t", 0))]
    out += [two(0, 0, ("sel", 0, k)) for k in range(4)]
    out += [two(0, 0, ("h", 0, k)) for k in range(4)]
    for j in range(PAIRS):
        if j == 0:
            out += [two(4, 1, ("x", 2)), two(4, 1, ("x", 3))]
        for k in range(4):
            if j == 0:
                out.append((("sel", 1, k), 2 + k % 2))
            if j and k == 0:
                out.append((("out", j - 1), 6))
            out.append(two(4, 1, ("ht", j, k)))
            if j and j % 2 == 0 and j + 3 < PAIRS and k == 1:
                out += [two(4, 1, ("x", j + 2)), two(4, 1, ("x", j + 3))]
        if j % 2 == 0 and j + 3 < PAIRS:
            out.append((("t", j // 2 + 1), 7))
        for k in range(4):
            if j + 1 < PAIRS:
                out.append((("h", j + 1, k), k % 2))
            if j + 2 < PAIRS:
                out.append((("sel", j + 2, k), 2 + k % 2))
    out.append((("out", PAIRS - 1), 6))
    return out


def xn_base(half):
    return PPH * (GROUPS * half - 1)


def x_tiles():
    out = []
    for s in range(FIRST_SLOT - 1, SLOTS + 3):
        for half in range(HALVES):
            j = s - xn_base(half)
            if 0 <= j < 4:
                out += [("ln", PPH * half + 2 * j, s), ("ln", PPH * half + 2 * j + 1, s)]
            p = s - 3 - PPH * (GROUPS * (half + 1) - 1)
            if 0 <= p < PPH:
                out.append(("res", PPH * half + p, s))
        if s == SLOTS - PPH - 1:
            out += [("ffn", 0, s), ("ffn", 1, s)]
    return out


def psw_uses():
    out = []
    for s in range(FIRST_SLOT, SLOTS + 2):
        if 0 <= s - 2 < SLOTS:
            out.append(("wo", s - 2))
        for half in range(HALVES):
            j = s - xn_base(half)
            if 0 <= j < 4:
                out += [("xn", PPH * half + 2 * j), ("xn", PPH * half + 2 * j + 1)]
    return out


def build(nc, x, ctx_t, bias, mask, gates, wq, wk, wv, wo, c1, c2, w1, w2, out):
    PIECES = pieces()
    piece_no = {(q[0], q[1]): n for n, q in enumerate(PIECES)}
    F_USES = ffn_uses()
    f_bank = dict(F_USES)
    f_before = {}
    last_in = {}
    for use, b in F_USES:
        f_before[use] = last_in.get(b)
        last_in[b] = use
    XT = x_tiles()
    xt_no = {(k, t): n for n, (k, t, _) in enumerate(XT)}
    PSW = psw_uses()
    psw_no = {u: n for n, u in enumerate(PSW)}
    n_psw = len(PSW)
    LN_TILES = PAIRS
    x1_dram = nc.dram_tensor("x1_between_halves", [PAIRS, P, D], F32, kind="Internal").ap()

    with ExitStack() as whole:
        def sb(stack, name, shape, dt):
            return stack.enter_context(nc.sbuf_tensor(name, shape, dt))

        def sem(name):
            return whole.enter_context(nc.semaphore(name))

        bank = [whole.enter_context(nc.psum_tensor(f"bank{i}", [P, 512], F32)) for i in range(8)]

        ident = sb(whole, "ident", [P, P], F32)
        raw = [sb(whole, f"raw{i}", [P, PIECE], F32) for i in range(RAW)]
        gate_in = sb(whole, "gate_in", [P, 2], F32)
        gate = sb(whole, "gate_tanh", [P, 2], F32)
        stats = [sb(whole, f"ln_stats{i}", [P, 6], F32) for i in range(2)]
        mv = [sb(whole, f"ln_mean_var{i}", [P, 2], F32) for i in range(2)]
        veps = [sb(whole, f"ln_var_eps{i}", [P, 1], F32) for i in range(2)]
        rstd = [sb(whole, f"ln_rstd{i}", [P, 1], F32) for i in range(2)]
        minus_half = sb(whole, "minus_half", [P, 1], F32)
        less_hi = sb(whole, "rows_less_hi", [P, 1], F32)
        xn = [sb(whole, f"xn{i}", [P, D], F32) for i in range(2)]

        rank_w = sb(whole, "earlier_is_larger", [P, SPARSITY], BF16)

        with ExitStack() as st:
            xnt = [sb(st, f"xnt_{n}", [P, CH, HTOK], F32R) for n in ("hi", "lo")]
            ctxt = [sb(st, f"ctxt_{n}", [P, CH, HTOK], F32R) for n in ("hi", "lo")]
            wkvq = {k: [sb(st, f"{k}_{n}", [P, CH, GC], F32R) for n in ("hi", "lo")]
                    for k in ("wk", "wv", "wq")}
            kt, v, bias_in = [None] * 2, [None] * 2, [None] * 2

            def per_iteration(i):
                kt[i] = sb(st, f"kt{i}", [P, HPG, HTOK], F32)
                if i:
                    qt[0] = sb(st, "qt", [P, HPG, HTOK], F32)
                v[i] = sb(st, f"v{i}", [P, PPH, GC], F32)
                bias_in[i] = sb(st, f"bias_in{i}", [P, PPH, HPG * S], F32)

            qt = [None]
            per_iteration(0)
            per_iteration(1)
            qt = qt[0]
            wo_s = [[sb(st, f"wo{i}_{n}", [P, HPG, D], F32R) for n in ("hi", "lo")] for i in range(2)]
            cxo = [[sb(st, f"attn_t{i}_{n}", [P, HPG, P], F32R) for n in ("hi", "lo")] for i in range(2)]
            mask_in = sb(st, "mask_in", [P, PAIRS, S], U8)
            mask_add = sb(st, "mask_add", [P, PAIRS, S], BF16)
            valid = sb(st, "row_has_key", [P, PAIRS], F32)
            bm = [sb(st, f"bias_mask{i}", [P, HPG, S], F32) for i in range(2)]
            sc = [sb(st, f"scores{i}", [P, HPG, S], F32) for i in range(2)]
            ex = [sb(st, f"exp{i}", [P, HPG, S], F32) for i in range(2)]
            negmax = [sb(st, f"negmax{i}", [P, HPG], F32) for i in range(2)]
            rsum = [sb(st, f"rowsum{i}", [P, HPG], F32) for i in range(2)]
            rinv = [sb(st, f"rowinv{i}", [P, HPG], F32) for i in range(2)]
            pb = [sb(st, f"probs_blockdiag{i}", [P, HPG, P], F32) for i in range(2)]
            pt = [sb(st, f"probs_t{i}", [P, HPG, P], F32) for i in range(2)]
            xt = [sb(st, f"x_tile{i}", [P, D], F32) for i in range(XR)]
            acc = sb(st, "attn_sum", [P, PPH, D], F32)

        with ExitStack() as st:
            w1s = [sb(st, f"w1_{n}", [P, CH * INTER], F32R) for n in ("hi", "lo")]
            c1s = [sb(st, f"c1_{n}", [P, CH, P], F32R) for n in ("hi", "lo")]
            c2s = sb(st, "c2_stacked", [P, INTER], F32R)
            xft, ts, x2 = [None] * 2, [None] * 2, [None] * X2R

            def per_unit(i):
                xft[i] = [sb(st, f"xft{i}_{n}", [P, CH, FU], F32R) for n in ("hi", "lo")]
                ts[i] = sb(st, f"low_rank_stacked{i}", [P, FU], F32R)
                x2[2 * i:2 * i + 2] = [sb(st, f"x1_tile{n}", [P, D], F32) for n in (2 * i, 2 * i + 1)]

            per_unit(0)
            pick = sb(st, "selector", [P, INTER], F32)
            is_max = sb(st, "is_max", [P, NBLK, SPARSITY], BF16)
            first = [sb(st, f"first_max{i}", [P, NBLK, SPARSITY], BF16) for i in range(2)]
            m1 = sb(st, "block_max", [P, NBLK], F32)
            m2 = sb(st, "block_first", [P, NBLK], BF16)
            hm = sb(st, "h_picked", [P, INTER], F32)
            per_unit(1)
            x2[4] = sb(st, "x1_tile4", [P, D], F32)
            hmt = [sb(st, f"h_picked_t_{n}", [P, IC, P], F32R) for n in ("hi", "lo")]
            w2s = sb(st, "w2_hi_lo_by_piece", [P, 7, 2, PIECE], F32R)

        raw_in = [sem(f"dma_raw{i}") for i in range(RAW)]
        bias_sem = [sem(f"dma_bias{i}") for i in range(2)]
        xt_in = [sem(f"dma_x{i}") for i in range(XR)]
        x2_in = [sem(f"dma_x1_{i}") for i in range(X2R)]
        mask_sem = sem("dma_mask")
        gate_sem = sem("dma_gate")
        x1_out = [sem(f"dma_x1_store{i}") for i in range(PPH)]
        out_sem = [sem(f"dma_out{i}") for i in range(X2R)]
        pe_proj = sem("pe_proj")
        pe_score = sem("pe_score")
        pe_pt = sem("pe_pt")
        pe_pv = sem("pe_pv")
        pe_psw = sem("pe_psw")
        act_proj = sem("act_proj")
        act_exp = sem("act_exp")
        act_pt = sem("act_pt")
        act_chi = sem("act_chi")
        act_xhi = sem("act_xhi")
        act_gate = sem("act_gate")
        dve_hi = sem("dve_hi")
        dve_lo = sem("dve_lo")
        act_hi = sem("act_hi")
        dve_s = sem("dve_s")
        dve_max = sem("dve_max")
        dve_p = sem("dve_p")
        dve_clo = sem("dve_clo")
        dve_psw = sem("dve_psw")
        dve_acc = sem("dve_acc")
        dve_stat = sem("dve_stat")
        dve_xn = sem("dve_xn")
        dve_step = sem("dve_step")
        dve_mask = sem("dve_mask")
        pool_c = sem("pool_const")
        pool_own = sem("pool_own")
        pool_bm = sem("pool_bm")
        pool_rstd = sem("pool_rstd")
        pool_lo = sem("pool_lo")
        pe_x = sem("pe_ffn_xt")
        pe_t = sem("pe_ffn_t")
        pe_i = sem("pe_ffn_inter")
        pe_h = sem("pe_ffn_h")
        pe_ht = sem("pe_ffn_ht")
        pe_ou = sem("pe_ffn_out")
        act_i = sem("act_ffn_inter")
        act_h = sem("act_ffn_ht_hi")
        act_fx = sem("act_ffn_xt_hi")
        dve_fx = sem("dve_ffn_xt_lo")
        dve_t = sem("dve_ffn_t")
        dve_e = sem("dve_ffn_ismax")
        pool_e = sem("pool_ffn_rank")
        dve_oh = sem("dve_ffn_first")
        dve_hm = sem("dve_ffn_hm")
        dve_hl = sem("dve_ffn_ht_lo")
        dve_o = sem("dve_ffn_out")

        block = whole.enter_context(nc.Block())

        def wait(eng, s, n):
            if n > 0:
                eng.wait_ge(s, n)

        def ring(eng, sems, n):
            eng.wait_ge(sems[n % len(sems)], 16 * (n // len(sems) + 1))

        def dest(kind, i):
            if kind == "ctx":
                return ctxt[0][:, i % CH, :], ctxt[1][:, i % CH, :]
            if kind in wkvq:
                return [t[:, :, :].rearrange("p a b -> p (a b)") for t in wkvq[kind]]
            if kind == "wo":
                return [t[:, :, :].rearrange("p a b -> p (a b)") for t in wo_s[i % 2]]
            if kind == "w1":
                return [t[:, i * PIECE:(i + 1) * PIECE] for t in w1s]
            if kind == "w2":
                return w2s[:, i, 0, :], w2s[:, i, 1, :]
            if kind == "c1":
                return [t[:, :, :].rearrange("p a b -> p (a b)") for t in c1s]
            a = i * PIECE
            b = min(a + PIECE, INTER)
            return c2s[:, a:b], c2s[:, a:b]

        def source(kind, i):
            if kind == "ctx":
                return ctx_t[i // CH, i % CH]
            if kind in ("wk", "wv", "wq", "wo"):
                return {"wk": wk, "wv": wv, "wq": wq, "wo": wo}[kind][i % GROUPS]
            if kind == "c1":
                return c1
            t = {"w1": w1, "w2": w2, "c2": c2}[kind]
            return t[:, i * PIECE:min((i + 1) * PIECE, t.shape[1])]

        def wait_dest_free(eng, kind, i):
            if kind == "ctx" and i >= CH:
                wait(eng, pe_proj, OUTS * (GROUPS - 1) + 8)
            if kind in wkvq:
                wait(eng, pe_proj, OUTS * (i - 1) + {"wk": 4, "wv": 8, "wq": 12}[kind])
            if kind == "wo" and i >= 2:
                wait(eng, pe_psw, psw_no[("wo", PPH * (i - 1) - 1)] + 1)
            if kind == "c1":
                wait_early_free(eng)
            if kind == "w2" and i == 0:
                wait_late_free(eng)
            if kind == "w2" and i == 4:
                for q in x1_out:
                    eng.wait_ge(q, 16 * HALVES)

        hi_sem = {"dve": dve_hi, "act": act_hi}
        lo_sem = {"dve": dve_lo, "pool": pool_lo}

        def pieces_to(n, column):
            return sum(q[column] == PIECES[n][column] for q in PIECES[:n + 1])

        def wait_hi(eng, n):
            wait(eng, hi_sem[PIECES[n][4]], pieces_to(n, 4))

        def wait_split(eng, n):
            wait(eng, lo_sem[PIECES[n][5]], pieces_to(n, 5))

        def wait_bank_free(eng, use):
            b = f_before[use]
            if b is None:
                bk = f_bank[use]
                wait(eng, (act_proj, act_proj, dve_s, dve_s, act_pt, dve_clo, dve_psw, dve_psw)[bk],
                     (OUTS * ITERS, OUTS * ITERS, SLOTS, SLOTS, SLOTS, SLOTS, n_psw, n_psw)[bk])
            elif b[0] in ("x", "t", "out"):
                wait(eng, {"x": dve_fx, "t": dve_t, "out": dve_o}[b[0]], b[1] + 1)
            else:
                wait(eng, {"sel": act_i, "h": dve_hm, "ht": dve_hl}[b[0]], 4 * b[1] + b[2] + 1)

        def wait_early_free(eng):
            wait(eng, pe_proj, OUTS * ITERS)
            wait(eng, pe_score, PPH * (ITERS - 1))
            wait(eng, pe_pv, PPH * (ITERS - 1))
            wait(eng, pool_bm, PPH * (ITERS - 1))

        def wait_k_q_free(eng):
            wait(eng, pe_score, SLOTS)

        def wait_late_free(eng):
            wait(eng, pe_psw, n_psw)
            wait(eng, dve_acc, PAIRS)

        @block.sync
        def _(sp):
            todo = []

            def add(slot, order, f):
                todo.append((slot, order, len(todo), f))

            def load_piece(n):
                kind, i, cols = PIECES[n][:3]
                if n >= RAW:
                    wait_split(sp, n - RAW)
                sp.dma_start(raw[n % RAW][:, 0:cols], source(kind, i)).then_inc(raw_in[n % RAW], 16)

            def load_x(n):
                kind, t, _ = XT[n]
                if n >= XR:
                    k0, t0, _ = XT[n - XR]
                    if k0 in ("ln", "ffn"):
                        wait(sp, dve_xn, t0 + 1 + (LN_TILES if k0 == "ffn" else 0))
                    else:
                        wait(sp, dve_acc, t0 + 1)
                if kind == "ffn":
                    sp.wait_ge(x1_out[t], 16)
                sp.dma_start(xt[n % XR][:, :], (x1_dram if kind == "ffn" else x)[t])\
                    .then_inc(xt_in[n % XR], 16)

            def load_bias(it):
                wait(sp, pool_bm, PPH * (it - 1))
                sp.dma_start(bias_in[it % 2][:, :, :], bias[it]).then_inc(bias_sem[it % 2], 16)

            def store_x1(t):
                wait(sp, dve_acc, t + 1)
                sp.dma_start(x1_dram[t], acc[:, t % PPH, :]).then_inc(x1_out[t % PPH], 16)

            def load_x2(t):
                if t >= X2R:
                    sp.wait_ge(out_sem[t % X2R], 16 * (t // X2R))
                elif t < 2:
                    wait_early_free(sp)
                elif t == 2:
                    wait_k_q_free(sp)
                sp.wait_ge(x1_out[t % PPH], 16 * (t // PPH + 1))
                sp.dma_start(x2[t % X2R][:, :], x1_dram[t]).then_inc(x2_in[t % X2R], 16)

            for t in range(2):
                add(PPH * (ITERS - 1), -1, lambda t=t: load_x2(t))
            for t in range(2, X2R):
                add(SLOTS, -1, lambda t=t: load_x2(t))
            add(-97, 0, lambda: sp.dma_start(mask_in[:, :, :], mask).then_inc(mask_sem, 16))
            for n in range(len(PIECES)):
                add(PIECES[n - RAW][3] if n >= RAW else -99, 0, lambda n=n: load_piece(n))
            for n in range(len(XT)):
                add(XT[n - XR][2] if n >= XR else -98, 1, lambda n=n: load_x(n))
            for it in range(ITERS):
                add(PPH * (it - 1), 2, lambda it=it: load_bias(it))
            for t in range(PAIRS):
                it = GROUPS * (t // PPH + 1) - 1
                add(PPH * it + t % PPH + 4, -2, lambda t=t: store_x1(t))
            todo.sort(key=lambda a: a[:3])
            for item in todo[:2 * RAW]:
                item[3]()
            sp.dma_start(gate_in[:, :], gates).then_inc(gate_sem, 16)
            for item in todo[2 * RAW:]:
                item[3]()
            for t in range(PAIRS):
                wait(sp, dve_o, t + 1)
                sp.dma_start(out[t], x2[t % X2R][:, :]).then_inc(out_sem[t % X2R], 16)
                if t + X2R < PAIRS:
                    load_x2(t + X2R)
            for k in range(X2R):
                sp.wait_ge(out_sem[k], 16 * len(range(k, PAIRS, X2R)))
            for k in range(PPH):
                sp.wait_ge(x1_out[k], 16 * HALVES)

        @block.gpsimd
        def _(pool):
            pool.memset(ident[:, :], 0.0).then_inc(pool_own, 1)
            for i in range(2):
                pool.memset(pb[i][:, :, :], 0.0).then_inc(pool_c, 1)
            pool.memset(minus_half[:, :], -0.5).then_inc(pool_c, 1)
            for t in range(SPARSITY):
                pool.memset(rank_w[:, t:t + 1], float(SPARSITY - t)).then_inc(pool_c, 1)
            wait(pool, pool_own, 1)
            pool.affine_select(out=ident[:, :], in_=ident[:, :], compare_op=ALU.not_equal, fill=1.0,
                               base=0, pattern=[[-1, P]], channel_multiplier=1).then_inc(pool_c, 1)
            own = [1]

            def do_rstd(n):
                wait(pool, dve_stat, n + 1)
                wait(pool, dve_xn, n - 1)
                pool.tensor_scalar(veps[n % 2][:, :], mv[n % 2][:, 1:2], EPS, None, ALU.add)\
                    .then_inc(pool_own, 1)
                own[0] += 1
                wait(pool, pool_own, own[0])
                pool.tensor_tensor(rstd[n % 2][:, :], veps[n % 2][:, :], minus_half[:, :], ALU.pow)\
                    .then_inc(pool_rstd, 1)

            def do_bm(s):
                it, p = divmod(s, PPH)
                if s == 0:
                    wait(pool, dve_mask, 2)
                if p == 0:
                    ring(pool, bias_sem, it)
                wait(pool, dve_s, s - 1)
                tile = PPH * (it // GROUPS) + p
                pool.tensor_tensor(
                    bm[s % 2][:, :, :], bias_in[it % 2][:, p, :].rearrange("p (h k) -> p h k", h=HPG),
                    mask_add[:, tile, :].unsqueeze(1).broadcast_to([P, HPG, S]), ALU.add)\
                    .then_inc(pool_bm, 1)

            def do_lo(n):
                kind, i, cols = PIECES[n][:3]
                hi, lo = dest(kind, i)
                wait_hi(pool, n)
                pool.tensor_tensor(lo, raw[n % RAW][:, 0:cols], hi.bitcast(F32), ALU.subtract)\
                    .then_inc(pool_lo, 1)

            def rank(t):
                wait(pool, dve_e, t + 1)
                pool.tensor_tensor(is_max[:, :, :], is_max[:, :, :],
                                   rank_w[:, :].unsqueeze(1).broadcast_to([P, NBLK, SPARSITY]), ALU.mult)\
                    .then_inc(pool_e, 1)

            n = 0
            for s in range(FIRST_SLOT - 1, SLOTS + 4):
                for k, t, slot in XT:
                    if k == "ln" and slot == s:
                        do_rstd(t)
                if s == SLOTS - PPH - 1:
                    do_rstd(LN_TILES)
                    do_rstd(LN_TILES + 1)
                if 0 <= s + 1 < SLOTS:
                    do_bm(s + 1)
                if s == SLOTS - 4:
                    rank(0)
                if s == SLOTS + 1:
                    do_rstd(LN_TILES + 2)
                    do_rstd(LN_TILES + 3)
                if s == SLOTS + 3:
                    rank(1)
                while n < len(PIECES) and PIECES[n][3] == s:
                    if PIECES[n][5] == "pool":
                        do_lo(n)
                    n += 1
            for j in range(PAIRS):
                if j % 2 and j + 4 < PAIRS:
                    do_rstd(LN_TILES + j + 3)
                    do_rstd(LN_TILES + j + 4)
                if j + 2 < PAIRS:
                    rank(j + 2)

        @block.scalar
        def _(act):
            n = [0]

            def his(s):
                while n[0] < len(PIECES) and PIECES[n[0]][3] == s:
                    kind, i, cols, _, by, _ = PIECES[n[0]]
                    if by == "act":
                        wait_dest_free(act, kind, i)
                        ring(act, raw_in, n[0])
                        act.activation(dest(kind, i)[0], raw[n[0] % RAW][:, 0:cols], ACT.Copy)\
                            .then_inc(act_hi, 1)
                    n[0] += 1

            his(FIRST_SLOT - 1)
            act.wait_ge(gate_sem, 16)
            act.activation(gate[:, :], gate_in[:, :], ACT.Tanh).then_inc(act_gate, 1)

            def evac(n):
                it, k = divmod(n, OUTS)
                wait(act, pe_proj, n + 1)
                b = bank[n % 2][:, :]
                if k < 4:
                    tb, h = divmod(k, HPG)
                    wait(act, pe_score, PPH * (it - 1))
                    o = kt[it % 2][:, h, tb * TB:(tb + 1) * TB]
                elif k < 8:
                    j = k - 4
                    wait(act, pe_pv, PPH * (it - 1))
                    o = v[it % 2][:, 2 * j:2 * j + 2, :].rearrange("p a b -> p (a b)")
                else:
                    tb, h = divmod(k - 8, HPG)
                    wait(act, pe_score, PPH * (it - 1) + (tb + 1) * (TB // P))
                    o = qt[:, h, tb * TB:(tb + 1) * TB]
                act.activation(o, b, ACT.Copy).then_inc(act_proj, 1)

            def exps(s):
                wait(act, dve_max, s + 1)
                wait(act, dve_p, s - 1)
                for h in range(HPG):
                    last = act.activation(ex[s % 2][:, h, :], sc[s % 2][:, h, :], ACT.Exp,
                                          bias=negmax[s % 2][:, h:h + 1], scale=1.0,
                                          accum_out=rsum[s % 2][:, h:h + 1])
                last.then_inc(act_exp, 1)

            def probs_t(s):
                wait(act, pe_pt, s + 1)
                wait(act, pe_pv, s - 1)
                act.activation(pt[s % 2][:, :, :].rearrange("p a b -> p (a b)"), bank[4][:, 0:HPG * P],
                               ACT.Copy).then_inc(act_pt, 1)

            def chi(s):
                wait(act, pe_pv, s + 1)
                if s >= 2:
                    wait(act, pe_psw, psw_no[("wo", s - 2)] + 1)
                act.activation(cxo[s % 2][0][:, :, :].rearrange("p a b -> p (a b)"),
                               bank[5][:, 0:HPG * P], ACT.Copy).then_inc(act_chi, 1)

            def xhi(t):
                n = psw_no[("xn", t)]
                wait(act, pe_psw, n + 1)
                if t >= PPH:
                    wait(act, pe_proj, OUTS * GROUPS)
                p = t % PPH
                act.activation(xnt[0][:, :, p * P:(p + 1) * P],
                               bank[6 + n % 2][:, :].rearrange("p (c t) -> p c t", c=CH),
                               ACT.Copy).then_inc(act_xhi, 1)

            def fx_hi(t):
                wait(act, pe_x, t + 1)
                wait(act, pe_h, 4 * (2 * (t // 2) - 2))
                u, a = divmod(t, 2)
                act.activation(xft[u % 2][0][:, :, a * P:(a + 1) * P],
                               bank[f_bank[("x", t)]][:, :].rearrange("p (c t) -> p c t", c=CH),
                               ACT.Copy).then_inc(act_fx, 1)

            def sel(t, k):
                wait(act, dve_e, t)
                a, w = IB[k]
                wait(act, pe_i, 4 * t + k + 1)
                act.activation(pick[:, a:a + w], bank[f_bank[("sel", t, k)]][:, 0:w], ACT.Copy)\
                    .then_inc(act_i, 1)

            def ht_hi(t, k):
                a, w = TGRP[k]
                wait(act, pe_ht, 4 * t + k + 1)
                if t:
                    wait(act, pe_ou, 4 * (t - 1) + k + 1)
                act.activation(hmt[0][:, a:a + w, :].rearrange("p a b -> p (a b)"),
                               bank[f_bank[("ht", t, k)]][:, 0:w * P], ACT.Copy).then_inc(act_h, 1)

            for s in range(FIRST_SLOT, SLOTS + 2):
                it, i = divmod(s, PPH)
                done = [None] * HUS
                if it + 1 < ITERS:
                    done = [OUTS * (it + 1) + (HUS * i + u) // 2 if (HUS * i + u) % 2 else None
                            for u in range(HUS)]
                for half in range(HALVES):
                    j = s - 1 - xn_base(half)
                    if 0 <= j < 4:
                        xhi(PPH * half + 2 * j)
                        xhi(PPH * half + 2 * j + 1)
                if done[0] is not None:
                    evac(done[0])
                if 0 <= s - 1 < SLOTS:
                    probs_t(s - 1)
                if 0 <= s < SLOTS:
                    exps(s)
                if done[1] is not None:
                    evac(done[1])
                if s == SLOTS - PPH + 4:
                    sel(0, 2)
                    sel(0, 3)
                if 0 <= s - 1 < SLOTS:
                    chi(s - 1)
                if done[2] is not None:
                    evac(done[2])
                if s == SLOTS - PPH + 1:
                    wait_early_free(act)
                    fx_hi(0)
                    fx_hi(1)
                if s == SLOTS - PPH + 3:
                    sel(0, 0)
                    sel(0, 1)
                his(s)

            wait_k_q_free(act)
            fx_hi(2)
            fx_hi(3)
            wait_late_free(act)
            for j in range(PAIRS):
                for k in range(4):
                    if j == 0:
                        sel(1, k)
                    ht_hi(j, k)
                    if j and j % 2 == 0 and j + 3 < PAIRS and k == 1:
                        fx_hi(j + 2)
                        fx_hi(j + 3)
                if j == 0:
                    his(SLOTS + 3)
                for k in range(4):
                    if j + 2 < PAIRS:
                        sel(j + 2, k)

        @block.vector
        def _(dve):
            step = [0]

            def link(ins):
                step[0] += 1
                ins.then_inc(dve_step, 1)
                return step[0]

            def after(n):
                dve.wait_ge(dve_step, n)

            sign_done = [0]

            def masks():
                for q in range(4):
                    sign_done[0] = link(dve.memset(less_hi[q * 32:(q + 1) * 32, :], -float(q % 2)))
                dve.wait_ge(mask_sem, 16)
                dve.tensor_scalar(mask_add[:, :, :], mask_in[:, :, :], -MASKED, MASKED, ALU.mult, ALU.add)\
                    .then_inc(dve_mask, 1)
                dve.tensor_reduce(valid[:, :], mask_in[:, :, :], AX.X, ALU.max).then_inc(dve_mask, 1)

            def split(n):
                kind, i, cols, _, by_hi, by_lo = PIECES[n]
                hi, lo = dest(kind, i)
                r = raw[n % RAW][:, 0:cols]
                if by_hi == "dve":
                    wait_dest_free(dve, kind, i)
                    ring(dve, raw_in, n)
                    dve.tensor_copy(hi, r).then_inc(dve_hi, 1)
                if by_lo == "dve":
                    wait_hi(dve, n)
                    if kind != "c2":
                        dve.tensor_tensor(lo, r, hi.bitcast(F32), ALU.subtract).then_inc(dve_lo, 1)
                        return
                    after(sign_done[0])
                    dve.scalar_tensor_tensor(out=lo, in0=hi.bitcast(F32), scalar=less_hi[:, :],
                                             in1=r, op0=ALU.mult, op1=ALU.add).then_inc(dve_lo, 1)

            def ln_stats(n, src):
                wait(dve, dve_xn, n - 1)
                wait(dve, pool_rstd, n - 1)
                a = link(dve.bn_stats(stats[n % 2][:, :], src))
                after(a)
                dve.bn_aggr(mv[n % 2][:, :], stats[n % 2][:, :]).then_inc(dve_stat, 1)

            def ln_norm(n, src, transposed, k):
                wait(dve, pool_rstd, n + 1)
                wait(dve, transposed, k)
                dve.tensor_scalar(xn[n % 2][:, :], src, mv[n % 2][:, 0:1], rstd[n % 2][:, :],
                                  ALU.subtract, ALU.mult).then_inc(dve_xn, 1)

            def scores(s):
                wait(dve, pe_score, s + 1)
                wait(dve, pool_bm, s + 1)
                wait(dve, act_exp, s - 1)
                dve.scalar_tensor_tensor(out=sc[s % 2][:, :, :],
                                         in0=bank[2 + s % 2][:, 0:HPG * S].rearrange("p (h k) -> p h k", h=HPG),
                                         scalar=SCALE, in1=bm[s % 2][:, :, :],
                                         op0=ALU.mult, op1=ALU.add).then_inc(dve_s, 1)
                wait(dve, dve_s, s + 1)
                dve.tensor_reduce(negmax[s % 2][:, :], sc[s % 2][:, :, :], AX.X, ALU.max, negate=True)\
                    .then_inc(dve_max, 1)

            def probs(s):
                tile = PPH * (s // PPH // GROUPS) + s % PPH
                wait(dve, act_exp, s + 1)
                a = link(dve.reciprocal(rinv[s % 2][:, :], rsum[s % 2][:, :]))
                after(a)
                wait(dve, pe_pt, s - 1)
                for q in range(2):
                    r = slice(q * S, (q + 1) * S)
                    last = dve.scalar_tensor_tensor(
                        out=pb[s % 2][r, :, q * S:(q + 1) * S], in0=ex[s % 2][r, :, :],
                        scalar=valid[r, tile:tile + 1],
                        in1=rinv[s % 2][r, :].unsqueeze(2).broadcast_to([S, HPG, S]),
                        op0=ALU.mult, op1=ALU.mult)
                last.then_inc(dve_p, 1)

            def clo(s):
                wait(dve, act_chi, s + 1)
                hi, lo = (t[:, :, :].rearrange("p a b -> p (a b)") for t in cxo[s % 2])
                dve.tensor_tensor(lo, bank[5][:, 0:HPG * P], hi.bitcast(F32), ALU.subtract)\
                    .then_inc(dve_clo, 1)

            def add_wo(s):
                it, p = divmod(s, PPH)
                tile = PPH * (it // GROUPS) + p
                n = psw_no[("wo", s)]
                wait(dve, pe_psw, n + 1)
                b = bank[6 + n % 2][:, :]
                if it % GROUPS == 0:
                    if it:
                        dve.wait_ge(x1_out[p], 16)
                    dve.tensor_copy(acc[:, p, :], b).then_inc(dve_psw, 1)
                    return
                dve.tensor_tensor(acc[:, p, :], acc[:, p, :], b, ALU.add).then_inc(dve_psw, 1)
                if it % GROUPS == GROUPS - 1:
                    m = xt_no[("res", tile)]
                    ring(dve, xt_in, m)
                    wait(dve, dve_psw, n + 1)
                    dve.scalar_tensor_tensor(out=acc[:, p, :], in0=acc[:, p, :], scalar=gate[:, 0:1],
                                             in1=xt[m % XR][:, :], op0=ALU.mult, op1=ALU.add)\
                        .then_inc(dve_acc, 1)

            def xlo(t):
                n = psw_no[("xn", t)]
                p = t % PPH
                wait(dve, act_xhi, t + 1)
                dve.tensor_tensor(xnt[1][:, :, p * P:(p + 1) * P],
                                  bank[6 + n % 2][:, :].rearrange("p (c t) -> p c t", c=CH),
                                  xnt[0][:, :, p * P:(p + 1) * P].bitcast(F32), ALU.subtract)\
                    .then_inc(dve_psw, 1)

            L = LN_TILES

            def f_ln(ts_):
                for t in ts_:
                    if t >= 2:
                        ring(dve, x2_in, t)
                        ln_stats(L + t, x2[t % X2R][:, :])
                    else:
                        ring(dve, xt_in, xt_no[("ffn", t)])
                        ln_stats(L + t, xt[xt_no[("ffn", t)] % XR][:, :])
                for t in ts_:
                    if t >= 2:
                        ln_norm(L + t, x2[t % X2R][:, :], pe_x, t - 1)
                    else:
                        ln_norm(L + t, xt[xt_no[("ffn", t)] % XR][:, :],
                                pe_psw, psw_no[("xn", PAIRS - 2 + t)] + 1)

            def fx_lo(t):
                u, a = divmod(t, 2)
                wait(dve, act_fx, t + 1)
                dve.tensor_tensor(xft[u % 2][1][:, :, a * P:(a + 1) * P],
                                  bank[f_bank[("x", t)]][:, :].rearrange("p (c t) -> p c t", c=CH),
                                  xft[u % 2][0][:, :, a * P:(a + 1) * P].bitcast(F32), ALU.subtract)\
                    .then_inc(dve_fx, 1)

            def low_rank(u):
                wait(dve, pe_t, u + 1)
                wait(dve, pe_i, 4 * 2 * (u - 1))
                b = bank[f_bank[("t", u)]]
                a = link(dve.tensor_copy(ts[u % 2][:, :], b[:, 0:FU]))
                after(a)
                dve.tensor_tensor(ts[u % 2][64:128, :], b[64:128, 0:FU],
                                  ts[u % 2][64:128, :].bitcast(F32), ALU.subtract).then_inc(dve_t, 1)

            blk = pick[:, :].rearrange("p (n k) -> p n k", k=SPARSITY)
            mx_done = [0]

            def block_max(t, k):
                a, w = IB[k]
                wait(dve, act_i, 4 * t + k + 1)
                mx_done[0] = link(dve.tensor_reduce(
                    m1[:, a // SPARSITY:(a + w) // SPARSITY],
                    blk[:, a // SPARSITY:(a + w) // SPARSITY, :], AX.X, ALU.max))

            def mark_max(t):
                after(mx_done[0])
                wait(dve, dve_oh, t)
                dve.tensor_tensor(is_max[:, :, :], blk, m1[:, :].unsqueeze(2).broadcast_to([P, NBLK, SPARSITY]),
                                  ALU.is_equal).then_inc(dve_e, 1)

            def block_rank(t):
                wait(dve, pool_e, t + 1)
                mx_done[0] = link(dve.tensor_reduce(m2[:, :], is_max[:, :, :], AX.X, ALU.max))

            def first_max(t):
                after(mx_done[0])
                wait(dve, dve_hm, 4 * (t - 1))
                dve.tensor_tensor(first[t % 2][:, :, :], is_max[:, :, :],
                                  m2[:, :].unsqueeze(2).broadcast_to([P, NBLK, SPARSITY]),
                                  ALU.is_equal).then_inc(dve_oh, 1)

            def pick_h(t, k):
                a, w = IB[k]
                wait(dve, pe_h, 4 * t + k + 1)
                wait(dve, dve_oh, t + 1)
                wait(dve, pe_ht, 4 * (t - 1) + 4)
                dve.scalar_tensor_tensor(
                    out=hm[:, a:a + w], in0=bank[f_bank[("h", t, k)]][:, 0:w], scalar=0.0,
                    in1=first[t % 2][:, :, :].rearrange("p a b -> p (a b)")[:, a:a + w],
                    op0=ALU.max, op1=ALU.mult).then_inc(dve_hm, 1)

            def ht_lo(t, k):
                a, w = TGRP[k]
                wait(dve, act_h, 4 * t + k + 1)
                hi, lo = (x[:, a:a + w, :].rearrange("p a b -> p (a b)") for x in hmt)
                dve.tensor_tensor(lo, bank[f_bank[("ht", t, k)]][:, 0:w * P], hi.bitcast(F32), ALU.subtract)\
                    .then_inc(dve_hl, 1)

            def finish(t):
                wait(dve, pe_ou, 4 * t + 4)
                if t < 2:
                    ring(dve, x2_in, t)
                dve.scalar_tensor_tensor(out=x2[t % X2R][:, :], in0=bank[6][:, :], scalar=gate[:, 1:2],
                                         in1=x2[t % X2R][:, :], op0=ALU.mult, op1=ALU.add)\
                    .then_inc(dve_o, 1)

            n = 0
            for s in range(FIRST_SLOT - 1, SLOTS + 4):
                before = [PPH * half + 2 * (s - 1 - xn_base(half)) for half in range(HALVES)
                          if 0 <= s - 1 - xn_base(half) < 4]
                if before:
                    if 0 <= s - 3 < SLOTS:
                        add_wo(s - 3)
                    xlo(before[0])
                    xlo(before[0] + 1)
                if 0 <= s < SLOTS:
                    scores(s)
                if s == FIRST_SLOT:
                    wait(dve, pool_c, POOL_CONSTS)
                    wait(dve, act_gate, 1)
                early = s - (SLOTS - PPH)
                if early == 7:
                    pick_h(0, 0)
                    pick_h(0, 1)
                if early in (9, 10):
                    pick_h(0, early - 7)
                if 0 <= s - 3 < SLOTS and not before:
                    add_wo(s - 3)
                ln = [(t, xt_no[("ln", t)]) for k, t, slot in XT if k == "ln" and slot == s]
                for t, m in ln:
                    ring(dve, xt_in, m)
                    ln_stats(t, xt[m % XR][:, :])
                for t, m in ln:
                    ln_norm(t, xt[m % XR][:, :], pe_psw, psw_no[("xn", t - 2)] + 1 if t >= 2 else 0)
                if 0 <= s < SLOTS:
                    probs(s)
                if early == 3:
                    low_rank(0)
                if early >= 0:
                    if s - 1 < SLOTS:
                        clo(s - 1)
                while n < len(PIECES) and PIECES[n][3] == s < SLOTS:
                    split(n)
                    n += 1
                if s == FIRST_SLOT + 4:
                    masks()
                if 0 <= s - 1 and early < 0:
                    clo(s - 1)
                if early == -1:
                    f_ln((0, 1))
                if early == 1:
                    fx_lo(0)
                    fx_lo(1)
                if s == SLOTS + 1:
                    f_ln((2, 3))
                if early == 4:
                    for k in range(4):
                        block_max(0, k)
                    mark_max(0)
                if early == 5:
                    block_rank(0)
                if early == 6:
                    first_max(0)

            fx_lo(2)
            fx_lo(3)
            for j in range(PAIRS):
                nxt = j + 1 < PAIRS
                prep = j % 2 == 0 and j + 3 < PAIRS
                if j == 0:
                    for k in range(4):
                        block_max(1, k)
                        ht_lo(0, k)
                        if k == 3:
                            mark_max(1)
                    low_rank(1)
                    while n < len(PIECES) - 3:
                        split(n)
                        n += 1
                    block_rank(1)
                    first_max(1)
                else:
                    ht_lo(j, 0)
                    ht_lo(j, 1)
                    if prep:
                        fx_lo(j + 2)
                        fx_lo(j + 3)
                    if nxt:
                        block_rank(j + 1)
                    ht_lo(j, 2)
                    if nxt:
                        first_max(j + 1)
                    ht_lo(j, 3)
                    if prep:
                        low_rank(j // 2 + 1)
                    finish(j - 1)
                for k in range(4):
                    if nxt:
                        pick_h(j + 1, k)
                    if j + 2 < PAIRS:
                        block_max(j + 2, k)
                    if j == 0 and k:
                        split(n)
                        n += 1
                    if k == 2 and j % 2 and j + 4 < PAIRS:
                        f_ln((j + 3, j + 4))
                if j + 2 < PAIRS:
                    mark_max(j + 2)
            finish(PAIRS - 1)

        @block.tensor
        def _(pe):
            def three(o, a, b, first_mm, last_mm):
                pe.matmul(o, a[0], b[0], start=first_mm, stop=False)
                pe.matmul(o, a[0], b[1], start=False, stop=False)
                return pe.matmul(o, a[1], b[0], start=False, stop=last_mm)

            def hi_lo(ts_, *idx):
                return [t[idx] for t in ts_]

            full = slice(None)

            def half_output(it, u):
                k, second = divmod(u, 2)
                n = OUTS * it + k
                b = bank[n % 2]
                if not second:
                    wait(pe, act_proj, n - 1)
                    if k % 4 == 0:
                        kind = ("wk", "wv", "wq")[k // 4]
                        wait_split(pe, piece_no[(kind, it)])
                        if k == 0 and it % GROUPS == 0:
                            wait_split(pe, piece_no[("ctx", CH * (it // GROUPS) + CH - 1)])
                        if k == 8 and it % GROUPS == 0:
                            wait(pe, dve_psw, psw_no[("xn", PPH * (it // GROUPS) + PPH - 1)] + 1)
                if 4 <= k < 8:
                    tile = 2 * (k - 4) + second
                    o = b[:, second * GC:(second + 1) * GC]
                    for c in range(CH):
                        mm = three(o, hi_lo(ctxt, full, c, slice(tile * P, (tile + 1) * P)),
                                   hi_lo(wkvq["wv"], full, c, full), c == 0, c == CH - 1)
                else:
                    w, xx = (wkvq["wk"], ctxt) if k < 4 else (wkvq["wq"], xnt)
                    tb, h = divmod(k % 4, HPG)
                    for c in (2 * second, 2 * second + 1):
                        mm = three(b[:, :], hi_lo(w, full, c, slice(h * DH, (h + 1) * DH)),
                                   hi_lo(xx, full, c, slice(tb * TB, (tb + 1) * TB)),
                                   c == 0, c == CH - 1)
                if second:
                    mm.then_inc(pe_proj, 1)

            def scores(s):
                it, p = divmod(s, PPH)
                if p == 0:
                    wait(pe, act_proj, OUTS * (it + 1))
                wait(pe, dve_s, s - 1)
                for q in range(2):
                    cols = slice(p * P + q * S, p * P + (q + 1) * S)
                    for h in range(HPG):
                        mm = pe.matmul(bank[2 + s % 2][q * S:(q + 1) * S, h * S:(h + 1) * S],
                                       qt[:, h, cols], kt[it % 2][:, h, cols], start=True, stop=True)
                mm.then_inc(pe_score, 1)

            def probs_t(s):
                wait(pe, dve_p, s + 1)
                wait(pe, act_pt, s)
                for h in range(HPG):
                    mm = pe.transpose(bank[4][:, h * P:(h + 1) * P], pb[s % 2][:, h, :], ident[:, :])
                mm.then_inc(pe_pt, 1)

            def attend(s):
                it, p = divmod(s, PPH)
                wait(pe, act_pt, s + 1)
                wait(pe, dve_clo, s)
                for h in range(HPG):
                    mm = pe.matmul(bank[5][:, h * P:(h + 1) * P], v[it % 2][:, p, h * DH:(h + 1) * DH],
                                   pt[s % 2][:, h, :], start=True, stop=True)
                mm.then_inc(pe_pv, 1)

            def project_out(s):
                it = s // PPH
                n = psw_no[("wo", s)]
                wait(pe, dve_psw, n - 1)
                if s % PPH == 0:
                    wait_split(pe, piece_no[("wo", it)])
                wait(pe, dve_clo, s + 1)
                for h in range(HPG):
                    mm = three(bank[6 + n % 2][:, :], hi_lo(cxo[s % 2], full, h, full),
                               hi_lo(wo_s[it % 2], full, h, full), h == 0, h == HPG - 1)
                mm.then_inc(pe_psw, 1)

            def transpose_x(t):
                n = psw_no[("xn", t)]
                wait(pe, dve_psw, n - 1)
                wait(pe, dve_xn, t + 1)
                for c in range(CH):
                    mm = pe.transpose(bank[6 + n % 2][:, c * P:(c + 1) * P], xn[t % 2][:, c * P:(c + 1) * P],
                                      ident[:, :])
                mm.then_inc(pe_psw, 1)

            def f_transpose_x(t):
                wait_bank_free(pe, ("x", t))
                wait(pe, dve_xn, LN_TILES + t + 1)
                for c in range(CH):
                    mm = pe.transpose(bank[f_bank[("x", t)]][:, c * P:(c + 1) * P],
                                      xn[t % 2][:, c * P:(c + 1) * P], ident[:, :])
                mm.then_inc(pe_x, 1)

            def low_rank(u):
                wait_bank_free(pe, ("t", u))
                wait(pe, dve_fx, 2 * u + 2)
                if u == 0:
                    wait_split(pe, piece_no[("c1", 0)])
                for c in range(CH):
                    mm = three(bank[f_bank[("t", u)]][:, 0:FU], hi_lo(c1s, full, c, full),
                               hi_lo(xft[u % 2], full, c, full), c == 0, c == CH - 1)
                mm.then_inc(pe_t, 1)

            def selector(t, k):
                u, a = divmod(t, 2)
                wait_bank_free(pe, ("sel", t, k))
                wait(pe, dve_t, u + 1)
                if t == 0 and k == 0:
                    wait_split(pe, piece_no[("c2", 1)])
                c0, w = IB[k]
                pe.matmul(bank[f_bank[("sel", t, k)]][:, 0:w], ts[u % 2][:, a * P:(a + 1) * P],
                          c2s[:, c0:c0 + w], start=True, stop=True).then_inc(pe_i, 1)

            def hidden(t, k, cs):
                u, a = divmod(t, 2)
                c0, w = IB[k]
                if cs[0] == 0:
                    wait_bank_free(pe, ("h", t, k))
                    wait(pe, dve_fx, t + 1)
                    if t == 0:
                        for n in range(c0 * CH // PIECE, (c0 + w) * CH // PIECE):
                            wait_split(pe, piece_no[("w1", n)])
                for c in cs:
                    col = c0 * CH + c * w
                    mm = three(bank[f_bank[("h", t, k)]][:, 0:w],
                               hi_lo(xft[u % 2], full, c, slice(a * P, (a + 1) * P)),
                               hi_lo(w1s, full, slice(col, col + w)), c == 0, c == CH - 1)
                if cs[-1] == CH - 1:
                    mm.then_inc(pe_h, 1)

            def transpose_h(t, k):
                a, w = TGRP[k]
                wait_bank_free(pe, ("ht", t, k))
                wait(pe, dve_hm, 4 * t + k + 1)
                for c in range(a, a + w):
                    mm = pe.transpose(bank[f_bank[("ht", t, k)]][:, (c - a) * P:(c - a + 1) * P],
                                      hm[:, c * P:(c + 1) * P], ident[:, :])
                mm.then_inc(pe_ht, 1)

            def output(t, k):
                a, w = TGRP[k]
                if k == 0:
                    wait_bank_free(pe, ("out", t))
                wait(pe, dve_hl, 4 * t + k + 1)
                if t == 0:
                    for n in range(a // 2, (a + w + 1) // 2):
                        wait_split(pe, piece_no[("w2", n)])
                for c in range(a, a + w):
                    o = (c % 2) * D
                    wh, wl = (w2s[:, c // 2, q, o:o + D] for q in range(2))
                    mm = three(bank[6][:, :], hi_lo(hmt, full, c, full), (wh, wl), c == 0, c == IC - 1)
                mm.then_inc(pe_ou, 1)

            def filler(i, u):
                if (i, u) == (0, 2):
                    f_transpose_x(0)
                    f_transpose_x(1)
                if (i, u) == (2, 2):
                    low_rank(0)
                if (i, u) in ((3, 2), (4, 0)):
                    selector(0, 4 - 2 * (u // 2) - 2)
                    selector(0, 4 - 2 * (u // 2) - 1)
                if i == 4 and u:
                    hidden(0, 0, (2 * u - 2, 2 * u - 1))
                if i == 6 and u:
                    hidden(0, 1, (2 * u - 2, 2 * u - 1))
                if i >= 8:
                    hidden(0, i - 6, ((0,), (1, 2), (3,))[u])

            wait(pe, pool_c, POOL_CONSTS)
            for s in range(FIRST_SLOT, SLOTS + 2):
                it, i = divmod(s, PPH)
                if it + 1 < ITERS:
                    unit = lambda u: half_output(it + 1, HUS * i + u)
                else:
                    unit = lambda u: filler(s - PPH * (ITERS - 1), u)
                last = s - (SLOTS - PPH)
                if 0 <= s < SLOTS and last <= 0:
                    scores(s)
                unit(0)
                if 0 <= s - 1 < SLOTS:
                    probs_t(s - 1)
                unit(1)
                if 0 <= s - 1 < SLOTS:
                    attend(s - 1)
                if 0 <= last < PPH - 1:
                    scores(s + 1)
                unit(2)
                if 0 <= s - 2 < SLOTS:
                    project_out(s - 2)
                for half in range(HALVES):
                    j = s - xn_base(half)
                    if 0 <= j < 4:
                        transpose_x(PPH * half + 2 * j)
                        transpose_x(PPH * half + 2 * j + 1)

            for j in range(PAIRS):
                prep = j % 2 == 0 and j + 3 < PAIRS
                if j == 0:
                    f_transpose_x(2)
                    f_transpose_x(3)
                for k in range(4):
                    if j == 0:
                        selector(1, k)
                    if j:
                        output(j - 1, k)
                    transpose_h(j, k)
                    if j and prep and k == 1:
                        f_transpose_x(j + 2)
                        f_transpose_x(j + 3)
                if prep:
                    low_rank(j // 2 + 1)
                for k in range(4):
                    if j + 1 < PAIRS:
                        hidden(j + 1, k, range(CH))
                    if j + 2 < PAIRS:
                        selector(j + 2, k)
            for k in range(4):
                output(PAIRS - 1, k)


_ORDER = ["x", "ctx_t", "bias", "mask", "gates", "wq", "wk", "wv", "wo", "c1", "c2", "w1", "w2"]


def layouts(a):
    def cols(w):
        return w.reshape(CH, P, GROUPS, GC).transpose(2, 1, 0, 3).reshape(GROUPS, P, CH * GC)

    gates = np.concatenate([np.broadcast_to(a["g_xattn"].reshape(1, 1), (P, 1)),
                            np.broadcast_to(a["g_ffn"].reshape(1, 1), (P, 1))], axis=1)
    bias = a["fside_Bx32xSxS2_0"].reshape(HALVES, PPH, 2, GROUPS, HPG, S, S)
    bias = bias.transpose(0, 3, 2, 5, 1, 4, 6).reshape(ITERS, P, PPH, HPG * S)
    mask = a["mask_BxSxS2_bk0"].reshape(PAIRS, P, S).transpose(1, 0, 2)
    c1 = np.zeros((D, 4, 32), np.float32)
    c1[:, :, :RANK] = a["L0_ffn_c1_w"].T[:, None, :]
    c2 = np.zeros((4, 32, INTER), np.float32)
    c2[:, :RANK, :] = a["L0_ffn_c2_w"].T[None]
    w1 = a["L0_ffn_w1"].T.reshape(CH, P, INTER).transpose(1, 0, 2)
    return {
        "x": a["x"].reshape(PAIRS, P, D),
        "ctx_t": a["ctx_4096"].reshape(B * S, D).T.reshape(CH, P, HALVES, HTOK).transpose(2, 0, 1, 3),
        "bias": bias,
        "mask": mask,
        "gates": gates,
        "wq": cols(a["L0_xattn_Wq"]),
        "wk": cols(a["L0_xattn_Wk"]),
        "wv": cols(a["L0_xattn_Wv"]),
        "wo": a["L0_xattn_Wo"].reshape(GROUPS, HPG, P, D).transpose(0, 2, 1, 3).reshape(GROUPS, P, HPG * D),
        "c1": c1.reshape(CH, P, P).transpose(1, 0, 2).reshape(P, CH * P),
        "c2": c2.reshape(P, INTER),
        "w1": np.concatenate([w1[:, :, c:c + w].reshape(P, CH * w) for c, w in IB], axis=1),
        "w2": a["L0_ffn_w2t"].reshape(IC, P, D).transpose(1, 0, 2).reshape(P, IC * D),
    }


def kernel(**inputs):
    import concourse.bacc as bacc
    from concourse.bass_utils import run_bass_kernel_spmd

    laid = layouts({k: np.asarray(v) for k, v in inputs.items()})
    nc = bacc.Bacc("TRN2", target_bir_lowering=False, num_devices=1)
    arrays, args = {}, []
    for name in _ORDER:
        a = np.ascontiguousarray(laid[name])
        arrays[f"in_{name}"] = a
        args.append(nc.dram_tensor(f"in_{name}", a.shape, mybir.dt.from_np(a.dtype), kind="ExternalInput").ap())
    out = nc.dram_tensor("out_0", [PAIRS, P, D], F32, kind="ExternalOutput").ap()
    build(nc, *args, out)
    r = run_bass_kernel_spmd(nc, [arrays], core_ids=[0])
    return r.results[0]["out_0"].reshape(B, S, D)
```

```python
from contextlib import ExitStack

import numpy as np

import concourse.bass as bass
from concourse import mybir

F32 = mybir.dt.float32
F32R = mybir.dt.float32r
BF16 = mybir.dt.bfloat16
U8 = mybir.dt.uint8
ALU = mybir.AluOpType
ACT = mybir.ActivationFunctionType
AX = mybir.AxisListType

B, S, D, H, DH = 32, 64, 512, 32, 128
INTER, SPARSITY, RANK = 1792, 32, 16
P = 128
PAIRS = B * S // P
HALVES = 2
PPH = PAIRS // HALVES
HTOK = PPH * P
HPG = 2
GROUPS = H // HPG
GC = HPG * DH
ITERS = HALVES * GROUPS
CH = D // P
TB = 512
NTB = HTOK // TB
OUTS = 12
OPB = OUTS // NTB
PPB = TB // P
HUS = 2 * OUTS // PPH
PIECE = 1024
RAW = 3
WARM_UP = 14
XR = 4
SCALE = float(np.float32(1.0) / np.sqrt(np.float32(DH)))
EPS = 1e-5
MASKED = -1e37
IC = INTER // P
NBLK = INTER // SPARSITY
IB = [(0, 512), (512, 512), (1024, 512), (1536, 256)]
TGRP = [(0, 4), (4, 4), (8, 4), (12, 2)]
X2R = 5
FU = 256
SLOTS = ITERS * PPH
LEAD = PPB
FIRST_SLOT = -LEAD
FILL = SLOTS - LEAD
POOL_CONSTS = 4 + SPARSITY


def pieces():
    out = [(*q, PIECE, FIRST_SLOT - 1, "act", "dve") for q in (("wk", 0), ("ctx", 0), ("ctx", 1))]
    out.append(("wv", 0, PIECE, FIRST_SLOT, "act", "dve"))
    for s in range(FIRST_SLOT, SLOTS + 1):
        it, i = divmod(s, PPH)
        for at, kind in ((2, "wk"), (3, "wv"), (4, "wq"), (6, "wo")):
            if i == at and it + 1 < ITERS:
                out.append((kind, it + 1, PIECE, s, "dve", "pool"))
        for half in range(HALVES):
            for c, at in enumerate((-9, -6, -3, -2) if half else (None, None, -3, -3)):
                if at is not None and s == PPH * GROUPS * half + at:
                    out.append(("ctx", CH * half + c, PIECE, s, "dve", "pool"))
        if s == FILL - 4:
            out.append(("c1", 0, CH * P, s, "act", "pool"))
        if s == FILL - 3:
            out.append(("c2", 0, PIECE, s, "act", "dve"))
        if s == FILL - 2:
            out.append(("c2", 1, INTER - PIECE, s, "act", "dve"))
        for n in {0: (0,), 1: (1, 2), 2: (3,), 3: (4,), 4: (5, 6)}.get(s - FILL, ()):
            out.append(("w1", n, PIECE, s, "act", "dve" if n in (1, 3) else "pool"))
    out += [("w2", n, PIECE, SLOTS + 3, "act", "pool" if n % 2 else "dve") for n in range(7)]
    return out


def ffn_uses():
    turn = [0, 0]

    def two(base, i, use):
        turn[i] += 1
        return (use, base + (turn[i] - 1) % 2)

    out = [two(0, 0, ("x", 0)), two(0, 0, ("x", 1)), two(0, 0, ("t", 0))]
    out += [two(0, 0, ("sel", 0, k)) for k in range(4)]
    out += [two(0, 0, ("h", 0, k)) for k in range(4)]
    out += [(("sel", 1, k), 2 + k % 2) for k in range(4)]
    for j in range(PAIRS):
        if j == 0:
            out += [two(4, 1, ("x", 2)), two(4, 1, ("x", 3))]
        for k in range(4):
            if j and k == 0:
                out.append((("out", j - 1), 6))
            out.append(two(4, 1, ("ht", j, k)))
            if j and j % 2 == 0 and j + 3 < PAIRS and k == 1:
                out += [(("x", j + 2), 7), two(4, 1, ("x", j + 3))]
        if j % 2 == 0 and j + 3 < PAIRS:
            out.append((("t", j // 2 + 1), 7))
        for k in range(4):
            if j + 1 < PAIRS:
                out.append((("h", j + 1, k), k % 2))
            if j + 2 < PAIRS:
                out.append((("sel", j + 2, k), 2 + k % 2))
    out.append((("out", PAIRS - 1), 7))
    return out


def xn_slots():
    at = [(-4, -3, -2, -1), (-8, -7, -3, -1)]
    return {PPH * GROUPS * half + a: PPH * half + 2 * j for half in range(HALVES)
            for j, a in enumerate(at[half])}


def x_tiles():
    out = []
    for s in range(FIRST_SLOT - 1, SLOTS + 3):
        if s in xn_slots():
            t = xn_slots()[s]
            out += [("ln", t, s), ("ln", t + 1, s)]
        for half in range(HALVES):
            p = s - 3 - PPH * (GROUPS * (half + 1) - 1)
            if 0 <= p < PPH:
                out.append(("res", PPH * half + p, s))
    return out


def psw_uses():
    out = []
    for s in range(FIRST_SLOT, SLOTS + 2):
        if 0 <= s - 2 < SLOTS:
            out.append(("wo", s - 2))
        if s in xn_slots():
            out += [("xn", xn_slots()[s]), ("xn", xn_slots()[s] + 1)]
    return out


def build(nc, x, ctx_t, bias, mask, gates, wq, wk, wv, wo, c1, c2, w1, w2, out):
    PIECES = pieces()
    piece_no = {(q[0], q[1]): n for n, q in enumerate(PIECES)}
    F_USES = ffn_uses()
    f_bank = dict(F_USES)
    f_before = {}
    last_in = {}
    for use, b in F_USES:
        f_before[use] = last_in.get(b)
        last_in[b] = use
    XT = x_tiles()
    XN = xn_slots()
    xt_no = {(k, t): n for n, (k, t, _) in enumerate(XT)}
    PSW = psw_uses()
    psw_no = {u: n for n, u in enumerate(PSW)}
    n_psw = len(PSW)
    LN_TILES = PAIRS
    x1_dram = nc.dram_tensor("x1_between_halves", [PAIRS, P, D], F32, kind="Internal").ap()

    with ExitStack() as whole:
        def sb(stack, name, shape, dt):
            return stack.enter_context(nc.sbuf_tensor(name, shape, dt))

        def sem(name):
            return whole.enter_context(nc.semaphore(name))

        bank = [whole.enter_context(nc.psum_tensor(f"bank{i}", [P, 512], F32)) for i in range(8)]

        ident = sb(whole, "ident", [P, P], F32)
        raw = [sb(whole, f"raw{i}", [P, PIECE], F32) for i in range(RAW)]
        gate_in = sb(whole, "gate_in", [P, 2], F32)
        gate = sb(whole, "gate_tanh", [P, 2], F32)
        stats = [sb(whole, f"ln_stats{i}", [P, 6], F32) for i in range(2)]
        mv = [sb(whole, f"ln_mean_var{i}", [P, 2], F32) for i in range(2)]
        veps = [sb(whole, f"ln_var_eps{i}", [P, 1], F32) for i in range(2)]
        rstd = [sb(whole, f"ln_rstd{i}", [P, 1], F32) for i in range(2)]
        minus_half = sb(whole, "minus_half", [P, 1], F32)
        less_hi = sb(whole, "rows_less_hi", [P, 1], F32)
        xn = [sb(whole, f"xn{i}", [P, D], F32) for i in range(2)]

        rank_w = sb(whole, "earlier_is_larger", [P, SPARSITY], BF16)

        c1s = [sb(whole, f"c1_{n}", [P, CH, P], F32R) for n in ("hi", "lo")]
        c2s = sb(whole, "c2_stacked", [P, INTER], F32R)
        xft, ts, x2 = [None] * 2, [None] * 2, [None] * X2R
        ts[0] = sb(whole, "low_rank_stacked0", [P, FU], F32R)
        x2[0:2] = [sb(whole, f"x1_tile{n}", [P, D], F32) for n in range(2)]

        with ExitStack() as st:
            xnt = [sb(st, f"xnt_{n}", [P, CH, HTOK], F32R) for n in ("hi", "lo")]
            ctxt = [sb(st, f"ctxt_{n}", [P, NTB, CH, TB], F32R) for n in ("hi", "lo")]
            wkvq = {k: [sb(st, f"{k}_{n}", [P, CH, GC], F32R) for n in ("hi", "lo")]
                    for k in ("wk", "wv", "wq")}
            bias_in = [sb(st, "bias_in0", [P, PPH, HPG * S], F32)]
            kt = sb(st, "kt", [P, HPG, HTOK], F32)
            qt = sb(st, "qt", [P, HPG, HTOK], F32)
            v = sb(st, "v", [P, PPH, 2, DH], F32)
            bias_in.append(sb(st, "bias_in1", [P, PPH, HPG * S], F32))
            wo_s = [[sb(st, f"wo{i}_{n}", [P, HPG, D], F32R) for n in ("hi", "lo")] for i in range(2)]
            cxo = [[sb(st, f"attn_t{i}_{n}", [P, HPG, P], F32R) for n in ("hi", "lo")] for i in range(2)]
            mask_in = sb(st, "mask_in", [P, PAIRS, S], U8)
            mask_add = sb(st, "mask_add", [P, PAIRS, S], BF16)
            valid = sb(st, "row_has_key", [P, PAIRS], F32)
            bm = [sb(st, f"bias_mask{i}", [P, HPG, S], F32) for i in range(2)]
            sc = [sb(st, f"scores{i}", [P, HPG, S], F32) for i in range(2)]
            ex = [sb(st, f"exp{i}", [P, HPG, S], F32) for i in range(2)]
            negmax = [sb(st, f"negmax{i}", [P, HPG], F32) for i in range(2)]
            rsum = [sb(st, f"rowsum{i}", [P, HPG], F32) for i in range(2)]
            rinv = [sb(st, f"rowinv{i}", [P, HPG], F32) for i in range(2)]
            pb = [sb(st, f"probs{i}", [P, HPG, S], F32) for i in range(2)]
            pt = [sb(st, f"probs_t{i}", [P, 2, HPG, S], F32) for i in range(2)]
            xt = [sb(st, f"x_tile{i}", [P, D], F32) for i in range(XR)]
            acc = sb(st, "attn_sum", [P, PPH, D], F32)

        with ExitStack() as st:
            w1s = [sb(st, f"w1_{n}", [P, CH * INTER], F32R) for n in ("hi", "lo")]
            xft[0] = [sb(st, f"xft0_{n}", [P, CH, FU], F32R) for n in ("hi", "lo")]
            pick = sb(st, "selector", [P, INTER], F32)
            is_max = sb(st, "is_max", [P, NBLK, SPARSITY], BF16)
            first = [sb(st, f"first_max{i}", [P, NBLK, SPARSITY], BF16) for i in range(2)]
            m1 = sb(st, "block_max", [P, NBLK], F32)
            m2 = sb(st, "block_first", [P, NBLK], BF16)
            hm = sb(st, "h_picked", [P, INTER], F32)
            xft[1] = [sb(st, f"xft1_{n}", [P, CH, FU], F32R) for n in ("hi", "lo")]
            ts[1] = sb(st, "low_rank_stacked1", [P, FU], F32R)
            x2[2:] = [sb(st, f"x1_tile{n}", [P, D], F32) for n in range(2, X2R)]
            hmt = [sb(st, f"h_picked_t_{n}", [P, IC, P], F32R) for n in ("hi", "lo")]
            w2s = sb(st, "w2_hi_lo_by_piece", [P, 7, 2, PIECE], F32R)

        raw_in = [sem(f"dma_raw{i}") for i in range(RAW)]
        bias_sem = [sem(f"dma_bias{i}") for i in range(2)]
        xt_in = [sem(f"dma_x{i}") for i in range(XR)]
        x2_in = [sem(f"dma_x1_{i}") for i in range(X2R)]
        mask_sem = sem("dma_mask")
        gate_sem = sem("dma_gate")
        x1_out = [sem(f"dma_x1_store{i}") for i in range(PPH)]
        out_sem = [sem(f"dma_out{i}") for i in range(X2R)]
        pe_proj = sem("pe_proj")
        pe_score = sem("pe_score")
        pe_pt = sem("pe_pt")
        pe_pv = sem("pe_pv")
        pe_psw = sem("pe_psw")
        act_proj = sem("act_proj")
        act_exp = sem("act_exp")
        act_pt = sem("act_pt")
        act_chi = sem("act_chi")
        act_xhi = sem("act_xhi")
        act_gate = sem("act_gate")
        dve_hi = sem("dve_hi")
        dve_lo = sem("dve_lo")
        act_hi = sem("act_hi")
        dve_s = sem("dve_s")
        dve_max = sem("dve_max")
        dve_p = sem("dve_p")
        dve_clo = sem("dve_clo")
        dve_psw = sem("dve_psw")
        dve_acc = sem("dve_acc")
        dve_stat = sem("dve_stat")
        dve_xn = sem("dve_xn")
        dve_step = sem("dve_step")
        dve_mask = sem("dve_mask")
        pool_c = sem("pool_const")
        pool_own = sem("pool_own")
        pool_bm = sem("pool_bm")
        pool_rstd = sem("pool_rstd")
        pool_lo = sem("pool_lo")
        pe_x = sem("pe_ffn_xt")
        pe_t = sem("pe_ffn_t")
        pe_i = sem("pe_ffn_inter")
        pe_h = sem("pe_ffn_h")
        pe_ht = sem("pe_ffn_ht")
        pe_ou = sem("pe_ffn_out")
        act_i = sem("act_ffn_inter")
        act_h = sem("act_ffn_ht_hi")
        act_fx = sem("act_ffn_xt_hi")
        dve_fx = sem("dve_ffn_xt_lo")
        dve_t = sem("dve_ffn_t")
        dve_e = sem("dve_ffn_ismax")
        pool_e = sem("pool_ffn_rank")
        dve_oh = sem("dve_ffn_first")
        dve_hm = sem("dve_ffn_hm")
        dve_hl = sem("dve_ffn_ht_lo")
        dve_o = sem("dve_ffn_out")

        block = whole.enter_context(nc.Block())

        def wait(eng, s, n):
            if n > 0:
                eng.wait_ge(s, n)

        def ring(eng, sems, n):
            eng.wait_ge(sems[n % len(sems)], 16 * (n // len(sems) + 1))

        def dest(kind, i):
            if kind == "ctx":
                return [t[:, :, :, :].rearrange("p a b c -> p (a b c)")[:, i % CH * PIECE:(i % CH + 1) * PIECE]
                        for t in ctxt]
            if kind in wkvq:
                return [t[:, :, :].rearrange("p a b -> p (a b)") for t in wkvq[kind]]
            if kind == "wo":
                return [t[:, :, :].rearrange("p a b -> p (a b)") for t in wo_s[i % 2]]
            if kind == "w1":
                return [t[:, i * PIECE:(i + 1) * PIECE] for t in w1s]
            if kind == "w2":
                return w2s[:, i, 0, :], w2s[:, i, 1, :]
            if kind == "c1":
                return [t[:, :, :].rearrange("p a b -> p (a b)") for t in c1s]
            a = i * PIECE
            b = min(a + PIECE, INTER)
            return c2s[:, a:b], c2s[:, a:b]

        def by_batch(t):
            return t[:, :, :].rearrange("p h (b q) -> p b h q", b=2)

        def source(kind, i):
            if kind == "ctx":
                return ctx_t[i // CH, i % CH]
            if kind in ("wk", "wv", "wq", "wo"):
                return {"wk": wk, "wv": wv, "wq": wq, "wo": wo}[kind][i % GROUPS]
            if kind == "c1":
                return c1
            t = {"w1": w1, "w2": w2, "c2": c2}[kind]
            return t[:, i * PIECE:min((i + 1) * PIECE, t.shape[1])]

        def wait_dest_free(eng, kind, i):
            if kind == "ctx" and i >= CH:
                wait(eng, pe_proj, OUTS * (GROUPS - 1) + OPB * (i % CH // 2) + 4)
            if kind in wkvq:
                wait(eng, pe_proj, OUTS * (i - 1) + OPB + {"wk": 2, "wv": 4, "wq": 6}[kind])
            if kind == "wo" and i >= 2:
                wait(eng, pe_psw, psw_no[("wo", PPH * (i - 1) - 1)] + 1)
            if kind == "w1" and i == 0:
                wait_early_free(eng)
            if kind == "w2" and i == 0:
                wait_late_free(eng)
            if kind == "w2" and i == 4:
                for q in x1_out:
                    eng.wait_ge(q, 16 * HALVES)

        hi_sem = {"dve": dve_hi, "act": act_hi}
        lo_sem = {"dve": dve_lo, "pool": pool_lo}

        def pieces_to(n, column):
            return sum(q[column] == PIECES[n][column] for q in PIECES[:n + 1])

        def wait_hi(eng, n):
            wait(eng, hi_sem[PIECES[n][4]], pieces_to(n, 4))

        def wait_split(eng, n):
            wait(eng, lo_sem[PIECES[n][5]], pieces_to(n, 5))

        def wait_bank_free(eng, use):
            b = f_before[use]
            if b is None:
                bk = f_bank[use]
                wait(eng, (act_proj, act_proj, dve_s, dve_s, act_pt, dve_clo, dve_psw, dve_psw)[bk],
                     (OUTS * ITERS, OUTS * ITERS, SLOTS, SLOTS, SLOTS, SLOTS, n_psw, n_psw)[bk])
            elif b[0] in ("x", "t", "out"):
                wait(eng, {"x": dve_fx, "t": dve_t, "out": dve_o}[b[0]], b[1] + 1)
            else:
                wait(eng, {"sel": act_i, "h": dve_hm, "ht": dve_hl}[b[0]], 4 * b[1] + b[2] + 1)

        def wait_early_free(eng):
            wait(eng, pe_proj, OUTS * ITERS)
            wait(eng, pool_bm, PPH * (ITERS - 1))

        def wait_k_q_free(eng):
            wait(eng, pe_score, SLOTS)

        def wait_late_free(eng):
            wait(eng, pe_psw, n_psw)
            wait(eng, dve_acc, PAIRS)

        @block.sync
        def _(sp):
            todo = []

            def add(slot, order, f):
                todo.append((slot, order, len(todo), f))

            def load_piece(n):
                kind, i, cols = PIECES[n][:3]
                if n >= RAW:
                    wait_split(sp, n - RAW)
                sp.dma_start(raw[n % RAW][:, 0:cols], source(kind, i)).then_inc(raw_in[n % RAW], 16)

            def load_x(n):
                kind, t, _ = XT[n]
                if n >= XR:
                    k0, t0, _ = XT[n - XR]
                    if k0 == "ln":
                        wait(sp, dve_xn, t0 + 1)
                    else:
                        wait(sp, dve_acc, t0 + 1)
                sp.dma_start(xt[n % XR][:, :], x[t]).then_inc(xt_in[n % XR], 16)

            def load_bias(it):
                wait(sp, pool_bm, PPH * (it - 1))
                sp.dma_start(bias_in[it % 2][:, :, :], bias[it]).then_inc(bias_sem[it % 2], 16)

            def store_x1(t):
                wait(sp, dve_acc, t + 1)
                sp.dma_start(x1_dram[t], acc[:, t % PPH, :]).then_inc(x1_out[t % PPH], 16)

            def load_x2(t):
                if t >= X2R:
                    sp.wait_ge(out_sem[t % X2R], 16 * (t // X2R))
                elif t == 2:
                    wait_k_q_free(sp)
                sp.wait_ge(x1_out[t % PPH], 16 * (t // PPH + 1))
                sp.dma_start(x2[t % X2R][:, :], x1_dram[t]).then_inc(x2_in[t % X2R], 16)

            for t in range(2):
                add(FILL - 4, -1, lambda t=t: load_x2(t))
            for t in range(2, X2R):
                add(SLOTS - 1, -1, lambda t=t: load_x2(t))
            add(FIRST_SLOT - 1, 2, lambda: sp.dma_start(mask_in[:, :, :], mask).then_inc(mask_sem, 16))
            for n in range(len(PIECES)):
                at = PIECES[n - RAW][3] if n >= RAW else -99
                if RAW + 2 <= n < 2 * RAW + 1:
                    at = FIRST_SLOT
                add(at, 0, lambda n=n: load_piece(n))
            for n in range(len(XT)):
                add(XT[n - XR][2] if n >= XR else FIRST_SLOT - 1 if n >= 2 else -98, 1, lambda n=n: load_x(n))
            for it in range(ITERS):
                add(PPH * (it - 1), 2, lambda it=it: load_bias(it))
            for t in range(PAIRS):
                it = GROUPS * (t // PPH + 1) - 1
                add(PPH * it + t % PPH + 4, -2, lambda t=t: store_x1(t))
            todo.sort(key=lambda a: a[:3])
            for item in todo[:2 * RAW]:
                item[3]()
            sp.dma_start(gate_in[:, :], gates).then_inc(gate_sem, 16)
            for item in todo[2 * RAW:]:
                item[3]()
            for t in range(PAIRS):
                wait(sp, dve_o, t + 1)
                sp.dma_start(out[t], x2[t % X2R][:, :]).then_inc(out_sem[t % X2R], 16)
                if t + X2R < PAIRS:
                    load_x2(t + X2R)
            for k in range(X2R):
                sp.wait_ge(out_sem[k], 16 * len(range(k, PAIRS, X2R)))
            for k in range(PPH):
                sp.wait_ge(x1_out[k], 16 * HALVES)

        @block.gpsimd
        def _(pool):
            pool.memset(ident[:, :], 0.0).then_inc(pool_own, 1)
            for i in range(2):
                pool.memset(pt[i][:, :, :, :], 0.0).then_inc(pool_c, 1)
            pool.memset(minus_half[:, :], -0.5).then_inc(pool_c, 1)
            for t in range(SPARSITY):
                pool.memset(rank_w[:, t:t + 1], float(SPARSITY - t)).then_inc(pool_c, 1)
            wait(pool, pool_own, 1)
            pool.affine_select(out=ident[:, :], in_=ident[:, :], compare_op=ALU.not_equal, fill=1.0,
                               base=0, pattern=[[-1, P]], channel_multiplier=1).then_inc(pool_c, 1)
            own = [1]

            def do_rstd(n):
                wait(pool, dve_stat, n + 1)
                wait(pool, dve_xn, n - 1)
                pool.tensor_scalar(veps[n % 2][:, :], mv[n % 2][:, 1:2], EPS, None, ALU.add)\
                    .then_inc(pool_own, 1)
                own[0] += 1
                wait(pool, pool_own, own[0])
                pool.tensor_tensor(rstd[n % 2][:, :], veps[n % 2][:, :], minus_half[:, :], ALU.pow)\
                    .then_inc(pool_rstd, 1)

            def do_bm(s):
                it, p = divmod(s, PPH)
                if s == 0:
                    wait(pool, dve_mask, 2)
                if p == 0:
                    ring(pool, bias_sem, it)
                wait(pool, dve_s, s - 1)
                tile = PPH * (it // GROUPS) + p
                pool.tensor_tensor(
                    bm[s % 2][:, :, :], bias_in[it % 2][:, p, :].rearrange("p (h k) -> p h k", h=HPG),
                    mask_add[:, tile, :].unsqueeze(1).broadcast_to([P, HPG, S]), ALU.add)\
                    .then_inc(pool_bm, 1)

            def do_lo(n):
                kind, i, cols = PIECES[n][:3]
                hi, lo = dest(kind, i)
                wait_hi(pool, n)
                pool.tensor_tensor(lo, raw[n % RAW][:, 0:cols], hi.bitcast(F32), ALU.subtract)\
                    .then_inc(pool_lo, 1)

            def rank(t):
                wait(pool, dve_e, t + 1)
                pool.tensor_tensor(is_max[:, :, :], is_max[:, :, :],
                                   rank_w[:, :].unsqueeze(1).broadcast_to([P, NBLK, SPARSITY]), ALU.mult)\
                    .then_inc(pool_e, 1)

            n = 0
            for s in range(FIRST_SLOT - 1, SLOTS + 4):
                for k, t, slot in XT:
                    if k == "ln" and slot == s:
                        do_rstd(t)
                if s == FILL - 1:
                    do_rstd(LN_TILES)
                    do_rstd(LN_TILES + 1)
                if 0 <= s + 1 < SLOTS:
                    do_bm(s + 1)
                if s == FILL + 3:
                    rank(0)
                if s == SLOTS:
                    do_rstd(LN_TILES + 2)
                    do_rstd(LN_TILES + 3)
                if s == SLOTS + 1:
                    rank(1)
                while n < len(PIECES) and PIECES[n][3] == s:
                    if PIECES[n][5] == "pool":
                        do_lo(n)
                    n += 1
            for j in range(PAIRS):
                if j % 2 and j + 4 < PAIRS:
                    do_rstd(LN_TILES + j + 3)
                    do_rstd(LN_TILES + j + 4)
                if j + 2 < PAIRS:
                    rank(j + 2)

        @block.scalar
        def _(act):
            n = [0]

            def his(s, most=len(PIECES)):
                end = n[0] + most
                while n[0] < min(len(PIECES), end) and PIECES[n[0]][3] == s:
                    kind, i, cols, _, by, _ = PIECES[n[0]]
                    if by == "act":
                        wait_dest_free(act, kind, i)
                        ring(act, raw_in, n[0])
                        act.activation(dest(kind, i)[0], raw[n[0] % RAW][:, 0:cols], ACT.Copy)\
                            .then_inc(act_hi, 1)
                    n[0] += 1

            his(FIRST_SLOT - 1)
            act.wait_ge(gate_sem, 16)
            act.activation(gate[:, :], gate_in[:, :], ACT.Tanh).then_inc(act_gate, 1)

            def evac(n):
                it, k = divmod(n, OUTS)
                wait(act, pe_proj, n + 1)
                b = bank[n % 2][:, :]
                tb, r = divmod(k, OPB)
                h = r % HPG
                cols = slice(tb * TB, (tb + 1) * TB)
                if r < 2:
                    wait(act, pe_score, PPH * (it - 1) + PPB * (tb + 1))
                    o = kt[:, h, cols]
                elif r < 4:
                    j = 2 * tb + h
                    wait(act, pe_pv, PPH * (it - 1) + 2 * j + 2)
                    for q in range(2):
                        b = bank[n % 2][q * S:(q + 1) * S, :].rearrange("p (t h d) -> p t h d", t=2, h=HPG)
                        for h in range(HPG):
                            last = act.activation(v[h * S:(h + 1) * S, 2 * j:2 * j + 2, q, :], b[:, :, h, :],
                                                  ACT.Copy)
                    last.then_inc(act_proj, 1)
                    return
                else:
                    wait(act, pe_score, PPH * (it - 1) + PPB * (tb + 1))
                    o = qt[:, h, cols]
                act.activation(o, b, ACT.Copy).then_inc(act_proj, 1)

            def exps(s):
                wait(act, dve_max, s + 1)
                wait(act, dve_p, s - 1)
                for h in range(HPG):
                    last = act.activation(ex[s % 2][:, h, :], sc[s % 2][:, h, :], ACT.Exp,
                                          bias=negmax[s % 2][:, h:h + 1], scale=1.0,
                                          accum_out=rsum[s % 2][:, h:h + 1])
                last.then_inc(act_exp, 1)

            def probs_t(s):
                wait(act, pe_pt, s + 1)
                wait(act, pe_pv, s - 1)
                for h in range(HPG):
                    rows = slice(h * S, (h + 1) * S)
                    last = act.activation(pt[s % 2][rows, :, h, :],
                                          bank[4][rows, 0:P].rearrange("p (b q) -> p b q", b=2), ACT.Copy)
                last.then_inc(act_pt, 1)

            def chi(s):
                wait(act, pe_pv, s + 1)
                if s >= 2:
                    wait(act, pe_psw, psw_no[("wo", s - 2)] + 1)
                act.activation(by_batch(cxo[s % 2][0]), bank[5][:, 0:HPG * P].rearrange(
                    "p (b h q) -> p b h q", b=2, h=HPG), ACT.Copy).then_inc(act_chi, 1)

            def xhi(t):
                n = psw_no[("xn", t)]
                wait(act, pe_psw, n + 1)
                if t >= PPH:
                    wait(act, pe_proj, OUTS * (GROUPS - 1) + OPB * (t % PPH // PPB + 1))
                p = t % PPH
                act.activation(xnt[0][:, :, p * P:(p + 1) * P],
                               bank[6 + n % 2][:, :].rearrange("p (c t) -> p c t", c=CH),
                               ACT.Copy).then_inc(act_xhi, 1)

            def fx_hi(t):
                wait(act, pe_x, t + 1)
                wait(act, pe_h, 4 * (2 * (t // 2) - 2))
                u, a = divmod(t, 2)
                act.activation(xft[u % 2][0][:, :, a * P:(a + 1) * P],
                               bank[f_bank[("x", t)]][:, :].rearrange("p (c t) -> p c t", c=CH),
                               ACT.Copy).then_inc(act_fx, 1)

            def sel(t, k):
                wait(act, dve_e, t)
                a, w = IB[k]
                wait(act, pe_i, 4 * t + k + 1)
                act.activation(pick[:, a:a + w], bank[f_bank[("sel", t, k)]][:, 0:w], ACT.Copy)\
                    .then_inc(act_i, 1)

            def ht_hi(t, k):
                a, w = TGRP[k]
                wait(act, pe_ht, 4 * t + k + 1)
                if t:
                    wait(act, pe_ou, 4 * (t - 1) + k + 1)
                act.activation(hmt[0][:, a:a + w, :].rearrange("p a b -> p (a b)"),
                               bank[f_bank[("ht", t, k)]][:, 0:w * P], ACT.Copy).then_inc(act_h, 1)

            for s in range(FIRST_SLOT, SLOTS + 2):
                first = HUS * (s + LEAD)
                done = [u // 2 if u % 2 and u < 2 * OUTS * ITERS else None
                        for u in range(first, first + HUS)]
                if s - 1 in XN:
                    xhi(XN[s - 1])
                    xhi(XN[s - 1] + 1)
                if done[0] is not None:
                    evac(done[0])
                if 0 <= s - 1 < SLOTS:
                    probs_t(s - 1)
                if 0 <= s < SLOTS:
                    exps(s)
                if done[1] is not None:
                    evac(done[1])
                if s == FILL + 2:
                    sel(0, 0)
                    sel(0, 1)
                if s >= FILL:
                    his(s, 1)
                if 0 <= s - 1 < SLOTS:
                    chi(s - 1)
                if done[2] is not None:
                    evac(done[2])
                if s == FILL:
                    wait_early_free(act)
                    fx_hi(0)
                    fx_hi(1)
                if s == FILL + 2:
                    sel(0, 2)
                    sel(0, 3)
                his(s)
                if s >= SLOTS:
                    sel(1, 2 * (s - SLOTS))
                    sel(1, 2 * (s - SLOTS) + 1)

            wait_k_q_free(act)
            fx_hi(2)
            fx_hi(3)
            wait_late_free(act)
            for j in range(PAIRS):
                for k in range(4):
                    ht_hi(j, k)
                    if j and j % 2 == 0 and j + 3 < PAIRS and k == 1:
                        fx_hi(j + 2)
                        fx_hi(j + 3)
                if j == 0:
                    his(SLOTS + 3, 3)
                for k in range(4):
                    if j + 2 < PAIRS:
                        sel(j + 2, k)
                    if j == 0:
                        his(SLOTS + 3, 1)

        @block.vector
        def _(dve):
            step = [0]

            def link(ins):
                step[0] += 1
                ins.then_inc(dve_step, 1)
                return step[0]

            def after(n):
                dve.wait_ge(dve_step, n)

            sign_done = [0]

            def masks():
                for q in range(4):
                    sign_done[0] = link(dve.memset(less_hi[q * 32:(q + 1) * 32, :], -float(q % 2)))
                dve.wait_ge(mask_sem, 16)
                dve.tensor_scalar(mask_add[:, :, :], mask_in[:, :, :], -MASKED, MASKED, ALU.mult, ALU.add)\
                    .then_inc(dve_mask, 1)
                dve.tensor_reduce(valid[:, :], mask_in[:, :, :], AX.X, ALU.max).then_inc(dve_mask, 1)

            def split(n):
                kind, i, cols, _, by_hi, by_lo = PIECES[n]
                hi, lo = dest(kind, i)
                r = raw[n % RAW][:, 0:cols]
                if by_hi == "dve":
                    wait_dest_free(dve, kind, i)
                    ring(dve, raw_in, n)
                    dve.tensor_copy(hi, r).then_inc(dve_hi, 1)
                if by_lo == "dve":
                    wait_hi(dve, n)
                    if kind != "c2":
                        dve.tensor_tensor(lo, r, hi.bitcast(F32), ALU.subtract).then_inc(dve_lo, 1)
                        return
                    after(sign_done[0])
                    dve.scalar_tensor_tensor(out=lo, in0=hi.bitcast(F32), scalar=less_hi[:, :],
                                             in1=r, op0=ALU.mult, op1=ALU.add).then_inc(dve_lo, 1)

            def ln_stats(n, src):
                wait(dve, dve_xn, n - 1)
                wait(dve, pool_rstd, n - 1)
                a = link(dve.bn_stats(stats[n % 2][:, :], src))
                after(a)
                dve.bn_aggr(mv[n % 2][:, :], stats[n % 2][:, :]).then_inc(dve_stat, 1)

            def ln_norm(n, src, transposed, k):
                wait(dve, pool_rstd, n + 1)
                wait(dve, transposed, k)
                dve.tensor_scalar(xn[n % 2][:, :], src, mv[n % 2][:, 0:1], rstd[n % 2][:, :],
                                  ALU.subtract, ALU.mult).then_inc(dve_xn, 1)

            def scores(s):
                wait(dve, pe_score, s + 1)
                wait(dve, pool_bm, s + 1)
                wait(dve, act_exp, s - 1)
                dve.scalar_tensor_tensor(out=sc[s % 2][:, :, :],
                                         in0=bank[2 + s % 2][:, 0:HPG * S].rearrange("p (h k) -> p h k", h=HPG),
                                         scalar=SCALE, in1=bm[s % 2][:, :, :],
                                         op0=ALU.mult, op1=ALU.add).then_inc(dve_s, 1)
                wait(dve, dve_s, s + 1)
                dve.tensor_reduce(negmax[s % 2][:, :], sc[s % 2][:, :, :], AX.X, ALU.max, negate=True)\
                    .then_inc(dve_max, 1)

            def probs(s):
                tile = PPH * (s // PPH // GROUPS) + s % PPH
                wait(dve, act_exp, s + 1)
                a = link(dve.reciprocal(rinv[s % 2][:, :], rsum[s % 2][:, :]))
                after(a)
                wait(dve, pe_pt, s - 1)
                dve.scalar_tensor_tensor(
                    out=pb[s % 2][:, :, :], in0=ex[s % 2][:, :, :], scalar=valid[:, tile:tile + 1],
                    in1=rinv[s % 2][:, :].unsqueeze(2).broadcast_to([P, HPG, S]),
                    op0=ALU.mult, op1=ALU.mult).then_inc(dve_p, 1)

            def clo(s):
                wait(dve, act_chi, s + 1)
                hi, lo = (by_batch(t) for t in cxo[s % 2])
                both = bank[5][:, 0:HPG * P].rearrange("p (b h q) -> p b h q", b=2, h=HPG)
                dve.tensor_tensor(lo, both, hi.bitcast(F32), ALU.subtract).then_inc(dve_clo, 1)

            def add_wo(s):
                it, p = divmod(s, PPH)
                tile = PPH * (it // GROUPS) + p
                n = psw_no[("wo", s)]
                wait(dve, pe_psw, n + 1)
                b = bank[6 + n % 2][:, :]
                if it % GROUPS == 0:
                    if it:
                        dve.wait_ge(x1_out[p], 16)
                    dve.tensor_copy(acc[:, p, :], b).then_inc(dve_psw, 1)
                    return
                dve.tensor_tensor(acc[:, p, :], acc[:, p, :], b, ALU.add).then_inc(dve_psw, 1)
                if it % GROUPS == GROUPS - 1:
                    m = xt_no[("res", tile)]
                    ring(dve, xt_in, m)
                    wait(dve, dve_psw, n + 1)
                    dve.scalar_tensor_tensor(out=acc[:, p, :], in0=acc[:, p, :], scalar=gate[:, 0:1],
                                             in1=xt[m % XR][:, :], op0=ALU.mult, op1=ALU.add)\
                        .then_inc(dve_acc, 1)

            def xlo(t):
                n = psw_no[("xn", t)]
                p = t % PPH
                wait(dve, act_xhi, t + 1)
                dve.tensor_tensor(xnt[1][:, :, p * P:(p + 1) * P],
                                  bank[6 + n % 2][:, :].rearrange("p (c t) -> p c t", c=CH),
                                  xnt[0][:, :, p * P:(p + 1) * P].bitcast(F32), ALU.subtract)\
                    .then_inc(dve_psw, 1)

            L = LN_TILES

            def f_ln(ts_):
                f_stats(ts_)
                f_norm(ts_)

            def f_stats(ts_):
                for t in ts_:
                    ring(dve, x2_in, t)
                    ln_stats(L + t, x2[t % X2R][:, :])

            def f_norm(ts_):
                for t in ts_:
                    if t >= 2:
                        ln_norm(L + t, x2[t % X2R][:, :], pe_x, t - 1)
                    else:
                        ln_norm(L + t, x2[t][:, :], pe_psw, psw_no[("xn", PAIRS - 2 + t)] + 1)

            def fx_lo(t):
                u, a = divmod(t, 2)
                wait(dve, act_fx, t + 1)
                dve.tensor_tensor(xft[u % 2][1][:, :, a * P:(a + 1) * P],
                                  bank[f_bank[("x", t)]][:, :].rearrange("p (c t) -> p c t", c=CH),
                                  xft[u % 2][0][:, :, a * P:(a + 1) * P].bitcast(F32), ALU.subtract)\
                    .then_inc(dve_fx, 1)

            def low_rank(u):
                wait(dve, pe_t, u + 1)
                wait(dve, pe_i, 4 * 2 * (u - 1))
                b = bank[f_bank[("t", u)]]
                a = link(dve.tensor_copy(ts[u % 2][:, :], b[:, 0:FU]))
                after(a)
                dve.tensor_tensor(ts[u % 2][64:128, :], b[64:128, 0:FU],
                                  ts[u % 2][64:128, :].bitcast(F32), ALU.subtract).then_inc(dve_t, 1)

            blk = pick[:, :].rearrange("p (n k) -> p n k", k=SPARSITY)
            mx_done = [0]

            def block_max(t, k):
                a, w = IB[k]
                wait(dve, act_i, 4 * t + k + 1)
                mx_done[0] = link(dve.tensor_reduce(
                    m1[:, a // SPARSITY:(a + w) // SPARSITY],
                    blk[:, a // SPARSITY:(a + w) // SPARSITY, :], AX.X, ALU.max))

            def mark_max(t):
                after(mx_done[0])
                wait(dve, dve_oh, t)
                dve.tensor_tensor(is_max[:, :, :], blk, m1[:, :].unsqueeze(2).broadcast_to([P, NBLK, SPARSITY]),
                                  ALU.is_equal).then_inc(dve_e, 1)

            def block_rank(t):
                wait(dve, pool_e, t + 1)
                mx_done[0] = link(dve.tensor_reduce(m2[:, :], is_max[:, :, :], AX.X, ALU.max))

            def first_max(t):
                after(mx_done[0])
                wait(dve, dve_hm, 4 * (t - 1))
                dve.tensor_tensor(first[t % 2][:, :, :], is_max[:, :, :],
                                  m2[:, :].unsqueeze(2).broadcast_to([P, NBLK, SPARSITY]),
                                  ALU.is_equal).then_inc(dve_oh, 1)

            def pick_h(t, k):
                a, w = IB[k]
                wait(dve, pe_h, 4 * t + k + 1)
                wait(dve, dve_oh, t + 1)
                wait(dve, pe_ht, 4 * (t - 1) + 4)
                dve.scalar_tensor_tensor(
                    out=hm[:, a:a + w], in0=bank[f_bank[("h", t, k)]][:, 0:w], scalar=0.0,
                    in1=first[t % 2][:, :, :].rearrange("p a b -> p (a b)")[:, a:a + w],
                    op0=ALU.max, op1=ALU.mult).then_inc(dve_hm, 1)

            def ht_lo(t, k):
                a, w = TGRP[k]
                wait(dve, act_h, 4 * t + k + 1)
                hi, lo = (x[:, a:a + w, :].rearrange("p a b -> p (a b)") for x in hmt)
                dve.tensor_tensor(lo, bank[f_bank[("ht", t, k)]][:, 0:w * P], hi.bitcast(F32), ALU.subtract)\
                    .then_inc(dve_hl, 1)

            def finish(t):
                wait(dve, pe_ou, 4 * t + 4)
                dve.scalar_tensor_tensor(out=x2[t % X2R][:, :], in0=bank[f_bank[("out", t)]][:, :],
                                         scalar=gate[:, 1:2],
                                         in1=x2[t % X2R][:, :], op0=ALU.mult, op1=ALU.add)\
                    .then_inc(dve_o, 1)

            n = 0
            for s in range(FIRST_SLOT - 1, SLOTS + 4):
                before = s - 1 in XN
                if before:
                    if 0 <= s - 3 < SLOTS:
                        add_wo(s - 3)
                    xlo(XN[s - 1])
                    xlo(XN[s - 1] + 1)
                if 0 <= s < SLOTS:
                    scores(s)
                if s == FIRST_SLOT:
                    wait(dve, pool_c, POOL_CONSTS)
                if s == 0:
                    wait(dve, act_gate, 1)
                early = s - FILL
                if 0 <= s - 3 < SLOTS and not before:
                    add_wo(s - 3)
                ln = [(t, xt_no[("ln", t)]) for k, t, slot in XT if k == "ln" and slot == s]
                for t, m in ln:
                    ring(dve, xt_in, m)
                    ln_stats(t, xt[m % XR][:, :])
                for t, m in ln:
                    ln_norm(t, xt[m % XR][:, :], pe_psw, psw_no[("xn", t - 2)] + 1 if t >= 2 else 0)
                if 0 <= s < SLOTS:
                    probs(s)
                if early >= 0 and s - 1 < SLOTS:
                    clo(s - 1)
                if early == 0:
                    fx_lo(0)
                    fx_lo(1)
                if early == 1:
                    low_rank(0)
                while n < len(PIECES) and PIECES[n][3] == s < SLOTS + 3:
                    split(n)
                    n += 1
                if s == FIRST_SLOT + 1:
                    masks()
                if 0 <= s - 1 and early < 0:
                    clo(s - 1)
                if early == -1:
                    f_ln((0, 1))
                if early == 2:
                    for k in range(4):
                        block_max(0, k)
                    mark_max(0)
                if early == 3:
                    block_rank(0)
                if early == 4:
                    f_stats((2, 3))
                    first_max(0)
                    pick_h(0, 0)
                    pick_h(0, 1)
                    f_norm((2, 3))
                    block_max(1, 0)
                    block_max(1, 1)
                if early == 5:
                    pick_h(0, 2)
                    pick_h(0, 3)

            fx_lo(2)
            fx_lo(3)
            block_max(1, 2)
            block_max(1, 3)
            for j in range(PAIRS):
                nxt = j + 1 < PAIRS
                prep = j % 2 == 0 and j + 3 < PAIRS
                if j == 0:
                    ht_lo(0, 0)
                    mark_max(1)
                    for k in range(1, 4):
                        ht_lo(0, k)
                    low_rank(1)
                    split(n)
                    split(n + 1)
                    n += 2
                    block_rank(1)
                    first_max(1)
                else:
                    ht_lo(j, 0)
                    ht_lo(j, 1)
                    if prep:
                        fx_lo(j + 2)
                        fx_lo(j + 3)
                    if nxt:
                        block_rank(j + 1)
                    ht_lo(j, 2)
                    if nxt:
                        first_max(j + 1)
                    ht_lo(j, 3)
                    if prep:
                        low_rank(j // 2 + 1)
                    finish(j - 1)
                for k in range(4):
                    if nxt:
                        pick_h(j + 1, k)
                    if j + 2 < PAIRS:
                        block_max(j + 2, k)
                    if j == 0:
                        for m in range(n, n + (2 if k == 0 else 1)):
                            split(m)
                        n += 2 if k == 0 else 1
                    if k == 2 and j % 2 and j + 4 < PAIRS:
                        f_ln((j + 3, j + 4))
                if j + 2 < PAIRS:
                    mark_max(j + 2)
            finish(PAIRS - 1)

        @block.tensor
        def _(pe):
            def three(o, a, b, first_mm, last_mm):
                pe.matmul(o, a[0], b[0], start=first_mm, stop=False)
                pe.matmul(o, a[0], b[1], start=False, stop=False)
                return pe.matmul(o, a[1], b[0], start=False, stop=last_mm)

            def hi_lo(ts_, *idx):
                return [t[idx] for t in ts_]

            full = slice(None)

            def half_output(it, u):
                k, second = divmod(u, 2)
                tb, r = divmod(k, OPB)
                n = OUTS * it + k
                b = bank[n % 2]
                if not second:
                    wait(pe, act_proj, n - 1)
                    if tb == 0 and r % 2 == 0:
                        wait_split(pe, piece_no[(("wk", "wv", "wq")[r // 2], it)])
                    if r == 0 and it % GROUPS == 0:
                        wait_split(pe, piece_no[("ctx", CH * (it // GROUPS) + 2 * tb + 1)])
                    if r == 4 and it % GROUPS == 0:
                        wait(pe, dve_psw, psw_no[("xn", PPH * (it // GROUPS) + PPB * (tb + 1) - 1)] + 1)
                if 2 <= r < 4:
                    o = b[:, second * GC:(second + 1) * GC]
                    cols = slice((2 * (r - 2) + second) * P, (2 * (r - 2) + second + 1) * P)
                    for c in range(CH):
                        mm = three(o, hi_lo(ctxt, full, tb, c, cols),
                                   hi_lo(wkvq["wv"], full, c, full), c == 0, c == CH - 1)
                else:
                    h = r % 2
                    for c in (2 * second, 2 * second + 1):
                        xx = (hi_lo(ctxt, full, tb, c, full) if r < 2 else
                              hi_lo(xnt, full, c, slice(tb * TB, (tb + 1) * TB)))
                        mm = three(b[:, :], hi_lo(wkvq["wk" if r < 2 else "wq"], full, c,
                                                  slice(h * DH, (h + 1) * DH)), xx, c == 0, c == CH - 1)
                if second:
                    mm.then_inc(pe_proj, 1)

            def scores(s):
                it, p = divmod(s, PPH)
                if p % PPB == 0:
                    wait(pe, act_proj, OUTS * it + OPB * (p // PPB + 1))
                wait(pe, dve_s, s - 1)
                for q in range(2):
                    cols = slice(p * P + q * S, p * P + (q + 1) * S)
                    for h in range(HPG):
                        mm = pe.matmul(bank[2 + s % 2][q * S:(q + 1) * S, h * S:(h + 1) * S],
                                       qt[:, h, cols], kt[:, h, cols], start=True, stop=True)
                mm.then_inc(pe_score, 1)

            def probs_t(s):
                wait(pe, dve_p, s + 1)
                wait(pe, act_pt, s)
                pe.transpose(bank[4][:, 0:P], pb[s % 2][:, :, :].rearrange("p h k -> p (h k)"),
                             ident[:, :]).then_inc(pe_pt, 1)

            def attend(s):
                it, p = divmod(s, PPH)
                wait(pe, act_pt, s + 1)
                wait(pe, dve_clo, s)
                for q in range(2):
                    mm = pe.matmul(bank[5][:, q * P:(q + 1) * P], v[:, p, q, :],
                                   pt[s % 2][:, q, :, :].rearrange("p h q -> p (h q)"),
                                   start=True, stop=True)
                mm.then_inc(pe_pv, 1)

            def project_out(s):
                it = s // PPH
                n = psw_no[("wo", s)]
                wait(pe, dve_psw, n - 1)
                if s % PPH == 0:
                    wait_split(pe, piece_no[("wo", it)])
                wait(pe, dve_clo, s + 1)
                for h in range(HPG):
                    mm = three(bank[6 + n % 2][:, :], hi_lo(cxo[s % 2], full, h, full),
                               hi_lo(wo_s[it % 2], full, h, full), h == 0, h == HPG - 1)
                mm.then_inc(pe_psw, 1)

            def transpose_x(t):
                n = psw_no[("xn", t)]
                wait(pe, dve_psw, n - 1)
                wait(pe, dve_xn, t + 1)
                for c in range(CH):
                    mm = pe.transpose(bank[6 + n % 2][:, c * P:(c + 1) * P], xn[t % 2][:, c * P:(c + 1) * P],
                                      ident[:, :])
                mm.then_inc(pe_psw, 1)

            def f_transpose_x(t):
                wait_bank_free(pe, ("x", t))
                wait(pe, dve_xn, LN_TILES + t + 1)
                for c in range(CH):
                    mm = pe.transpose(bank[f_bank[("x", t)]][:, c * P:(c + 1) * P],
                                      xn[t % 2][:, c * P:(c + 1) * P], ident[:, :])
                mm.then_inc(pe_x, 1)

            def low_rank(u):
                wait_bank_free(pe, ("t", u))
                wait(pe, dve_fx, 2 * u + 2)
                if u == 0:
                    wait_split(pe, piece_no[("c1", 0)])
                for c in range(CH):
                    mm = three(bank[f_bank[("t", u)]][:, 0:FU], hi_lo(c1s, full, c, full),
                               hi_lo(xft[u % 2], full, c, full), c == 0, c == CH - 1)
                mm.then_inc(pe_t, 1)

            def selector(t, k):
                u, a = divmod(t, 2)
                wait_bank_free(pe, ("sel", t, k))
                wait(pe, dve_t, u + 1)
                if t == 0 and k == 0:
                    wait_split(pe, piece_no[("c2", 1)])
                c0, w = IB[k]
                pe.matmul(bank[f_bank[("sel", t, k)]][:, 0:w], ts[u % 2][:, a * P:(a + 1) * P],
                          c2s[:, c0:c0 + w], start=True, stop=True).then_inc(pe_i, 1)

            def hidden(t, k, cs):
                u, a = divmod(t, 2)
                c0, w = IB[k]
                if cs[0] == 0:
                    wait_bank_free(pe, ("h", t, k))
                    wait(pe, dve_fx, t + 1)
                    if t == 0:
                        for n in range(c0 * CH // PIECE, (c0 + w) * CH // PIECE):
                            wait_split(pe, piece_no[("w1", n)])
                for c in cs:
                    col = c0 * CH + c * w
                    mm = three(bank[f_bank[("h", t, k)]][:, 0:w],
                               hi_lo(xft[u % 2], full, c, slice(a * P, (a + 1) * P)),
                               hi_lo(w1s, full, slice(col, col + w)), c == 0, c == CH - 1)
                if cs[-1] == CH - 1:
                    mm.then_inc(pe_h, 1)

            def transpose_h(t, k):
                a, w = TGRP[k]
                wait_bank_free(pe, ("ht", t, k))
                wait(pe, dve_hm, 4 * t + k + 1)
                for c in range(a, a + w):
                    mm = pe.transpose(bank[f_bank[("ht", t, k)]][:, (c - a) * P:(c - a + 1) * P],
                                      hm[:, c * P:(c + 1) * P], ident[:, :])
                mm.then_inc(pe_ht, 1)

            def output(t, k):
                a, w = TGRP[k]
                if k == 0:
                    wait_bank_free(pe, ("out", t))
                wait(pe, dve_hl, 4 * t + k + 1)
                if t == 0:
                    for n in range(a // 2, (a + w + 1) // 2):
                        wait_split(pe, piece_no[("w2", n)])
                for c in range(a, a + w):
                    o = (c % 2) * D
                    wh, wl = (w2s[:, c // 2, q, o:o + D] for q in range(2))
                    mm = three(bank[f_bank[("out", t)]][:, :], hi_lo(hmt, full, c, full), (wh, wl),
                               c == 0, c == IC - 1)
                mm.then_inc(pe_ou, 1)

            def filler(i, u):
                if (i, u) == (0, 2):
                    f_transpose_x(0)
                    f_transpose_x(1)
                if (i, u) == (1, 2):
                    low_rank(0)
                if i == 2 and u in (0, 2):
                    selector(0, u)
                    selector(0, u + 1)
                if i == 3 and 0 < u < 3:
                    hidden(0, 0, (2 * u - 2, 2 * u - 1))
                if i == 4 and 0 < u < 3:
                    hidden(0, 1, (2 * u - 2, 2 * u - 1))
                if i in (4, 5) and u == 3:
                    selector(1, 2 * i - 8)
                    selector(1, 2 * i - 7)
                if i == 5 and u == 3:
                    f_transpose_x(2)
                    f_transpose_x(3)
                    hidden(0, 2, range(CH))
                    hidden(0, 3, range(CH))

            wait(pe, pool_c, POOL_CONSTS)
            for _ in range(WARM_UP):
                pe.matmul(bank[7][:, 0:P], ident[:, :], ident[:, :], start=True, stop=True)
            for s in range(FIRST_SLOT, SLOTS + 2):
                def unit(u):
                    n = HUS * (s + LEAD) + u
                    if n < 2 * OUTS * ITERS:
                        half_output(*divmod(n, 2 * OUTS))
                    else:
                        filler(s - FILL, u)

                last = s - FILL
                if 0 <= s < SLOTS and last <= 0 and s % 2 == 0:
                    scores(s)
                    scores(s + 1)
                unit(0)
                if 0 <= s - 1 < SLOTS:
                    probs_t(s - 1)
                unit(1)
                if 0 <= s - 1 < SLOTS:
                    attend(s - 1)
                if last > 0 and s + 1 < SLOTS:
                    scores(s + 1)
                unit(2)
                if 0 <= s - 2 < SLOTS:
                    project_out(s - 2)
                if s >= SLOTS:
                    unit(3)
                if s in XN:
                    transpose_x(XN[s])
                    transpose_x(XN[s] + 1)

            for j in range(PAIRS):
                prep = j % 2 == 0 and j + 3 < PAIRS
                for k in range(4):
                    if j:
                        output(j - 1, k)
                    transpose_h(j, k)
                    if j and prep and k == 1:
                        f_transpose_x(j + 2)
                        f_transpose_x(j + 3)
                if prep:
                    low_rank(j // 2 + 1)
                for k in range(4):
                    if j + 1 < PAIRS:
                        hidden(j + 1, k, range(CH))
                    if j + 2 < PAIRS:
                        selector(j + 2, k)
            for k in range(4):
                output(PAIRS - 1, k)


_ORDER = ["x", "ctx_t", "bias", "mask", "gates", "wq", "wk", "wv", "wo", "c1", "c2", "w1", "w2"]


def layouts(a):
    def cols(w):
        return w.reshape(CH, P, GROUPS, GC).transpose(2, 1, 0, 3).reshape(GROUPS, P, CH * GC)

    gates = np.concatenate([np.broadcast_to(a["g_xattn"].reshape(1, 1), (P, 1)),
                            np.broadcast_to(a["g_ffn"].reshape(1, 1), (P, 1))], axis=1)
    bias = a["fside_Bx32xSxS2_0"].reshape(HALVES, PPH, 2, GROUPS, HPG, S, S)
    bias = bias.transpose(0, 3, 2, 5, 1, 4, 6).reshape(ITERS, P, PPH, HPG * S)
    mask = a["mask_BxSxS2_bk0"].reshape(PAIRS, P, S).transpose(1, 0, 2)
    c1 = np.zeros((D, 4, 32), np.float32)
    c1[:, :, :RANK] = a["L0_ffn_c1_w"].T[:, None, :]
    c2 = np.zeros((4, 32, INTER), np.float32)
    c2[:, :RANK, :] = a["L0_ffn_c2_w"].T[None]
    w1 = a["L0_ffn_w1"].T.reshape(CH, P, INTER).transpose(1, 0, 2)
    return {
        "x": a["x"].reshape(PAIRS, P, D),
        "ctx_t": a["ctx_4096"].reshape(B * S, D).T.reshape(2, 2, P, HALVES, NTB, TB)
        .transpose(3, 4, 0, 2, 1, 5).reshape(HALVES, CH, P, PIECE),
        "bias": bias,
        "mask": mask,
        "gates": gates,
        "wq": cols(a["L0_xattn_Wq"]),
        "wk": cols(a["L0_xattn_Wk"]),
        "wv": cols(a["L0_xattn_Wv"]),
        "wo": a["L0_xattn_Wo"].reshape(GROUPS, HPG, P, D).transpose(0, 2, 1, 3).reshape(GROUPS, P, HPG * D),
        "c1": c1.reshape(CH, P, P).transpose(1, 0, 2).reshape(P, CH * P),
        "c2": c2.reshape(P, INTER),
        "w1": np.concatenate([w1[:, :, c:c + w].reshape(P, CH * w) for c, w in IB], axis=1),
        "w2": a["L0_ffn_w2t"].reshape(IC, P, D).transpose(1, 0, 2).reshape(P, IC * D),
    }


def kernel(**inputs):
    import concourse.bacc as bacc
    from concourse.bass_utils import run_bass_kernel_spmd

    laid = layouts({k: np.asarray(v) for k, v in inputs.items()})
    nc = bacc.Bacc("TRN2", target_bir_lowering=False, num_devices=1)
    arrays, args = {}, []
    for name in _ORDER:
        a = np.ascontiguousarray(laid[name])
        arrays[f"in_{name}"] = a
        args.append(nc.dram_tensor(f"in_{name}", a.shape, mybir.dt.from_np(a.dtype), kind="ExternalInput").ap())
    out = nc.dram_tensor("out_0", [PAIRS, P, D], F32, kind="ExternalOutput").ap()
    build(nc, *args, out)
    r = run_bass_kernel_spmd(nc, [arrays], core_ids=[0])
    return r.results[0]["out_0"].reshape(B, S, D)
```
